# Optimizing a Trainium2 kernel written in Bass

```python
import numpy as np
import jax
import jax.numpy as jnp

def _softmax(x, axis=-1):
    return jax.nn.softmax(x, axis=axis)

def _gelu(x):
    return jax.nn.gelu(x, approximate=True)

def _silu(x):
    return jax.nn.silu(x)

def _sigmoid(x):
    return jax.nn.sigmoid(x)

def _layernorm(x, axis=-1, eps=1e-05):
    m = jnp.mean(x, axis=axis, keepdims=True)
    v = jnp.var(x, axis=axis, keepdims=True)
    return (x - m) / jnp.sqrt(v + eps)

def _scatter_add(tgt, idx, src, axis=0):
    return tgt.at[idx].add(src)

def _segment_sum(src, seg, n):
    return jax.ops.segment_sum(src, seg, n)
kernel_name = 'mk_adaln_d1_jaxref_r8_5b7c06'

def setup_inputs(seed: int=0):
    np.random.seed(seed)
    _w = jnp.asarray

    def _L0_attn_setup():
        import jax, jax.numpy as jnp
        import numpy as np
        B, L, D, S, K, FF = (2, 512, 128, 16, 3, 336)
        EPS = 1e-06

        def rmsnorm(x, w):
            var = jnp.mean(x * x, axis=-1, keepdims=True)
            return x * jax.lax.rsqrt(var + EPS) * w
        key = jax.random.key(seed)
        ks = jax.random.split(key, 12)
        return {'u': jax.random.normal(ks[0], (B, L, D), jnp.float32), 'pre_norm_w': jnp.ones((D,), jnp.float32), 'in_proj_w': jax.random.normal(ks[1], (3 * D, D), jnp.float32) * D ** (-0.5), 'short_w': jax.random.normal(ks[2], (3 * D, 1, K), jnp.float32) * 0.3, 'short_b': jax.random.normal(ks[3], (3 * D,), jnp.float32) * 0.02, 'log_poles': -(jax.random.uniform(ks[4], (D, S, 1), jnp.float32) * 0.3 + 0.001), 'residues': jax.random.normal(ks[5], (D, S), jnp.float32) * S ** (-0.5), 'D_skip': jax.random.normal(ks[6], (D,), jnp.float32) * 0.02, 'out_proj_w': jax.random.normal(ks[7], (D, D), jnp.float32) * D ** (-0.5), 'post_norm_w': jnp.ones((D,), jnp.float32), 'l1_w': jax.random.normal(ks[8], (FF, D), jnp.float32) * D ** (-0.5), 'l2_w': jax.random.normal(ks[9], (FF, D), jnp.float32) * D ** (-0.5), 'l3_w': jax.random.normal(ks[10], (D, FF), jnp.float32) * FF ** (-0.5)}
    _L0_attn_in = _L0_attn_setup()

    def _L0_ffn_setup():
        import jax, jax.numpy as jnp
        import numpy as np
        D_MODEL = 128
        HIDDEN = 512
        N_ROUTING = 2
        key = jax.random.key(seed)
        ks = jax.random.split(key, 10)
        s = 0.02
        x = jax.random.normal(ks[0], (4, 512, D_MODEL), dtype=jnp.float32)
        gate_w = jax.random.normal(ks[1], (N_ROUTING, D_MODEL), dtype=jnp.float32) * s
        w1 = jax.random.normal(ks[2], (N_ROUTING, D_MODEL, HIDDEN), dtype=jnp.float32) * s
        b1 = jax.random.normal(ks[3], (N_ROUTING, HIDDEN), dtype=jnp.float32) * s
        w2 = jax.random.normal(ks[4], (N_ROUTING, HIDDEN, D_MODEL), dtype=jnp.float32) * s
        b2 = jax.random.normal(ks[5], (N_ROUTING, D_MODEL), dtype=jnp.float32) * s
        sw1 = jax.random.normal(ks[6], (D_MODEL, HIDDEN), dtype=jnp.float32) * s
        sb1 = jax.random.normal(ks[7], (HIDDEN,), dtype=jnp.float32) * s
        sw2 = jax.random.normal(ks[8], (HIDDEN, D_MODEL), dtype=jnp.float32) * s
        sb2 = jax.random.normal(ks[9], (D_MODEL,), dtype=jnp.float32) * s
        return {'x': x, 'gate_w': gate_w, 'w1': w1, 'b1': b1, 'w2': w2, 'b2': b2, 'sw1': sw1, 'sb1': sb1, 'sw2': sw2, 'sb2': sb2}
    _L0_ffn_in = _L0_ffn_setup()
    _L0_c = _w((lambda *s: np.random.randn(*s).astype(np.float32) * 0.05)(32, 128))
    _L0_wmod = _w((lambda *s: np.random.randn(*s).astype(np.float32) * 0.05)(128, 6 * 128) * 128 ** (-0.5))
    _d = {'L0_attn_u': _L0_attn_in['u'], 'L0_attn_pre_norm_w': _L0_attn_in['pre_norm_w'], 'L0_attn_in_proj_w': _L0_attn_in['in_proj_w'], 'L0_attn_short_w': _L0_attn_in['short_w'], 'L0_attn_short_b': _L0_attn_in['short_b'], 'L0_attn_log_poles': _L0_attn_in['log_poles'], 'L0_attn_residues': _L0_attn_in['residues'], 'L0_attn_D_skip': _L0_attn_in['D_skip'], 'L0_attn_out_proj_w': _L0_attn_in['out_proj_w'], 'L0_attn_post_norm_w': _L0_attn_in['post_norm_w'], 'L0_attn_l1_w': _L0_attn_in['l1_w'], 'L0_attn_l2_w': _L0_attn_in['l2_w'], 'L0_attn_l3_w': _L0_attn_in['l3_w'], 'L0_ffn_gate_w': _L0_ffn_in['gate_w'], 'L0_ffn_w1': _L0_ffn_in['w1'], 'L0_ffn_b1': _L0_ffn_in['b1'], 'L0_ffn_w2': _L0_ffn_in['w2'], 'L0_ffn_b2': _L0_ffn_in['b2'], 'L0_ffn_sw1': _L0_ffn_in['sw1'], 'L0_ffn_sb1': _L0_ffn_in['sb1'], 'L0_ffn_sw2': _L0_ffn_in['sw2'], 'L0_ffn_sb2': _L0_ffn_in['sb2'], 'L0_c': _L0_c, 'L0_wmod': _L0_wmod}
    _x0 = _d['L0_attn_u']
    _d['L0_attn_u'] = jax.random.normal(jax.random.fold_in(jax.random.key(seed), 1), (32, 256, 128), dtype=_x0.dtype)
    del _x0
    return _d

def reference(L0_attn_u, L0_attn_pre_norm_w, L0_attn_in_proj_w, L0_attn_short_w, L0_attn_short_b, L0_attn_log_poles, L0_attn_residues, L0_attn_D_skip, L0_attn_out_proj_w, L0_attn_post_norm_w, L0_attn_l1_w, L0_attn_l2_w, L0_attn_l3_w, L0_ffn_gate_w, L0_ffn_w1, L0_ffn_b1, L0_ffn_w2, L0_ffn_b2, L0_ffn_sw1, L0_ffn_sb1, L0_ffn_sw2, L0_ffn_sb2, L0_c, L0_wmod):

    def _L0_attn_ref(u, pre_norm_w, in_proj_w, short_w, short_b, log_poles, residues, D_skip, out_proj_w, post_norm_w, l1_w, l2_w, l3_w):
        import jax, jax.numpy as jnp
        import numpy as np
        B, L, D, S, K, FF = (2, 512, 128, 16, 3, 336)
        EPS = 1e-06

        def rmsnorm(x, w):
            var = jnp.mean(x * x, axis=-1, keepdims=True)
            return x * jax.lax.rsqrt(var + EPS) * w
        Lc = u.shape[1]
        z = rmsnorm(u, pre_norm_w) @ in_proj_w.T
        zc = z.transpose(0, 2, 1)
        z_pre = jax.lax.conv_general_dilated(zc, short_w, window_strides=(1,), padding=[(K - 1, 0)], dimension_numbers=('NCH', 'OIH', 'NCH'), feature_group_count=3 * D)
        z_pre = z_pre + short_b[None, :, None]
        x2, x1, v = jnp.split(z_pre, 3, axis=1)
        t = jnp.arange(Lc, dtype=jnp.float32)
        h = jnp.sum(residues[:, :, None] * jnp.exp(log_poles * t[None, None, :]), axis=1)
        xv = x1 * v
        n = 2 * Lc
        Xf = jnp.fft.rfft(xv, n=n)
        Hf = jnp.fft.rfft(h, n=n)
        yconv = jnp.fft.irfft(Xf * Hf[None], n=n)[..., :Lc]
        y = (yconv + xv * D_skip[None, :, None]) * x2
        y = y.transpose(0, 2, 1)
        y = y @ out_proj_w.T + u
        zm = rmsnorm(y, post_norm_w)
        mlp = jax.nn.gelu(zm @ l1_w.T) * (zm @ l2_w.T) @ l3_w.T
        return y + mlp

    def _L0_ffn_ref(x, gate_w, w1, b1, w2, b2, sw1, sb1, sw2, sb2):
        import jax, jax.numpy as jnp
        import numpy as np
        D_MODEL = 128
        HIDDEN = 512
        N_ROUTING = 2
        B, S, D = x.shape
        xf = x.reshape(-1, D)
        gate_scores = xf @ gate_w.T
        gate_probs = jax.nn.softmax(gate_scores, axis=-1)
        top1 = jnp.argmax(gate_probs, axis=-1)
        one_hot = jax.nn.one_hot(top1, N_ROUTING, dtype=xf.dtype)
        masked = xf[None, :, :] * one_hot.T[:, :, None]
        h = jax.nn.relu(jnp.einsum('end,edh->enh', masked, w1) + b1[:, None, :])
        expert_out = jnp.einsum('enh,ehd->end', h, w2) + b2[:, None, :]
        routing_output = expert_out.sum(axis=0)
        shared = jax.nn.relu(xf @ sw1 + sb1) @ sw2 + sb2
        return (routing_output + shared).reshape(B, S, D)
    x = L0_attn_u
    mod = (_silu(L0_c) @ L0_wmod).reshape(L0_c.shape[0], 6, 1, -1)
    sa, ca, ga, sb, cb, gb = (mod[:, 0], mod[:, 1], mod[:, 2], mod[:, 3], mod[:, 4], mod[:, 5])
    ga = (2 * (ga >= 0) - 1) * jnp.maximum(jnp.abs(ga), 0.25)
    gb = (2 * (gb >= 0) - 1) * jnp.maximum(jnp.abs(gb), 0.25)
    h = _layernorm(x, axis=-1) * (1 + ca) + sa
    x = x + ga * _L0_attn_ref(h, L0_attn_pre_norm_w, L0_attn_in_proj_w, L0_attn_short_w, L0_attn_short_b, L0_attn_log_poles, L0_attn_residues, L0_attn_D_skip, L0_attn_out_proj_w, L0_attn_post_norm_w, L0_attn_l1_w, L0_attn_l2_w, L0_attn_l3_w)
    h = _layernorm(x, axis=-1) * (1 + cb) + sb
    x = x + gb * _L0_ffn_ref(h, L0_ffn_gate_w, L0_ffn_w1, L0_ffn_b1, L0_ffn_w2, L0_ffn_b2, L0_ffn_sw1, L0_ffn_sb1, L0_ffn_sw2, L0_ffn_sb2)
    return x

_drawn_inputs = setup_inputs


def setup_inputs(seed=0):
    import zlib

    import numpy as np

    out = dict(_drawn_inputs(seed))
    spreads = {'L0_attn_pre_norm_w': (1.0, 0.2), 'L0_attn_post_norm_w': (1.0, 0.2)}
    factors = {'L0_attn_short_b': 6.381,
     'L0_attn_D_skip': 30.778,
     'L0_ffn_gate_w': 4.705,
     'L0_ffn_w1': 4.013,
     'L0_ffn_b1': 8.0,
     'L0_ffn_w2': 3.286,
     'L0_ffn_b2': 7.859,
     'L0_ffn_sw1': 4.058,
     'L0_ffn_sb1': 8.0,
     'L0_ffn_sw2': 3.283,
     'L0_ffn_sb2': 8.0}
    for name, (base, spread) in spreads.items():
        noise = np.random.default_rng([zlib.crc32(name.encode()), seed]).standard_normal(out[name].shape)
        drawn = base * np.exp(spread * noise) if base else spread * noise
        out[name] = jnp.asarray(drawn.astype(out[name].dtype))
    for name, factor in factors.items():
        out[name] = (out[name] * factor).astype(out[name].dtype)
    return out
```

```python
from contextlib import ExitStack

import concourse.bass as bass
from concourse import mybir

F32 = mybir.dt.float32
BF16 = mybir.dt.bfloat16
ALU = mybir.AluOpType
ACT = mybir.ActivationFunctionType
ds = bass.ds

P = 128
LN_EPS = 1e-5
RMS_EPS = 1e-6
TILES = 4
GT = TILES * P


def pack_columns(widths):
    at, out = 0, {}
    for name, w in widths:
        out[name] = (at, at + w)
        at += w
    return out, at


def setup_columns(batch, poles, length):
    return pack_columns([("cT", batch), ("wmod", 6 * P), ("residues", poles), ("log_poles", poles), ("d_skip", 1),
                         ("short_w", 9), ("short_b", 3), ("pre_w", 1), ("post_w", 1), ("gate", 2),
                         ("ident", P), ("time", length)])


def weight_columns(ff, hidden):
    return pack_columns([("out", P), ("l1", ff), ("l2", ff), ("up", 3 * hidden), ("down", 3 * hidden), ("up_b", 3 * hidden // P)])


def adaln_block(nc, x, setup, win, weights, l3w, b2, out, batch, length, poles, ff, hidden):
    TOK = batch * length
    NG = TOK // GT
    NT = TOK // P
    SEQ = GT // length
    FFC = 3
    FW = ff // FFC
    UP = 3 * hidden // P
    CG = 8
    NCG = P // CG
    PARTS = 3
    REG = PARTS * CG * NT
    HW = 3 * P
    SLOTS = 4
    assert length == 2 * P and ff % FFC == 0 and FW <= P and NCG % SLOTS == 0
    sc, setup_w = setup_columns(batch, poles, length)
    wc, weights_w = weight_columns(ff, hidden)
    MOD = 7

    with ExitStack() as ctx:
        def sb(name, shape, dt=F32):
            return ctx.enter_context(nc.sbuf_tensor(name, shape, dt))

        def sem(name):
            return ctx.enter_context(nc.semaphore(name))

        bank = [ctx.enter_context(nc.psum_tensor(f"bank{i}", [P, 512], F32)) for i in range(8)]
        filt_dram = nc.dram_tensor("filter_parts", [P, PARTS * HW], BF16)
        mod_dram = nc.dram_tensor("modulation", [batch, MOD * P], F32)

        cst = sb("cst", [P, setup_w])
        win_sb = sb("win_sb", [P, 3 * P])
        w_sb = sb("w_sb", [P, weights_w])
        l3_sb = sb("l3_sb", [FW, FFC * P])
        gate_sb = sb("gate_sb", [P, P])
        res = sb("res", [P, TOK])
        x2T = sb("x2T", [P, TOK])
        xv = sb("xv", [P, NCG * REG], BF16)
        y_all = xv[:, :].bitcast(F32)
        toep_w = CG * PARTS * 2 * P
        big = sb("big", [P, SLOTS * toep_w // 2])
        toep = big[:, :].bitcast(BF16)

        def C(name):
            return cst[:, sc[name][0]:sc[name][1]]

        def W(name):
            return w_sb[:, wc[name][0]:wc[name][1]]

        ident = C("ident")

        silu_c = sb("silu_c", [P, batch])
        small = sb("small", [P, 64])
        mod1 = sb("mod1", [P, SEQ * 2 * P])
        stats1 = sb("stats1", [P, TILES * 6])
        mv1 = sb("mv1", [P, TILES * 2])
        rstd1 = sb("rstd1", [P, TILES])
        cent = sb("cent", [P, GT])
        sumsq1 = sb("sumsq1", [P, TILES])
        rms1 = sb("rms1", [P, TILES])
        half = sb("half", [P, TILES])
        hnorm = sb("hnorm", [P, GT])
        hT = sb("hT", [P, GT])
        acc1 = sb("acc1", [P, GT])
        accv = sb("accv", [P, GT])
        xvT = sb("xvT", [P, GT])
        rest = sb("rest", [P, GT])
        junk = sb("junk", [P, GT], BF16)

        decay = [y_all[:, i * length:(i + 1) * length] for i in range(4)]
        filt = y_all[:, 4 * length:5 * length]
        filt_r = [y_all[:, (5 + i) * length:(6 + i) * length] for i in range(2)]
        filt_p = xv[:, 14 * length:14 * length + PARTS * HW]
        mod_at = 8 * length * 2
        mod_sb = y_all[0:batch, mod_at:mod_at + MOD * P]
        bias2 = y_all[0:batch, mod_at + MOD * P:mod_at + (MOD + 3) * P]
        sign = y_all[0:batch, mod_at + (MOD + 3) * P:mod_at + (MOD + 5) * P]

        at = [0]

        def part(width, rows=P):
            at[0] += width
            return big[0:rows, at[0] - width:at[0]]

        hid = part(UP * GT)
        mlp = part(FFC * GT, FW)
        yx, y2, znorm, zT = part(GT), part(GT), part(GT), part(GT)
        yc = hnorm
        hn2, h2T, h2T1, h2T0 = acc1, accv, xvT, hT
        xin = rest[:, :]
        xin3 = xin.rearrange("p (t c) -> p t c", c=P)
        ffo2 = sb("ffo2", [P, GT])[:, :]
        mod3 = sb("mod3", [P, SEQ * 4 * P])
        modg = mod1[:, 0:SEQ * P]

        names = """setup_in win_in w_in x_in0 x_in1 mod_out filt_out silu mod_mm mod_ps mod_a mod_b mod_c mod_ready bias2_in half_set
        decay_done filt_acc filt_d filt_1 filt_2 filt_3 filt_4 filt_5 filt_ready win_scaled w_scaled gate_set
        mod1_in bn1 mvar1 veps1 rstd1_s cent_s h_s sumsq1_s meps1 rms1_s hnorm_s trh hT_s z_s acc_s tap1 conv_s
        xvT_s trx xv1_s rest_s xv2_s rest_free
        conv_mm y_act y_dve
        yc_s trY yx_s up_mm up_act up_dve outp y2_s sumsq2 meps2 rms2 znorm_s trZ zT_s gelu_s mlp_s l3_mm a_s ag_s xn_s
        bn2 mvar2 veps2 rstd2_s cent2 h2_s trH h2T_s router x1_s x0_s down_mm down_free addb fin xin_in mod3_in modg_in stored""".split()
        S = {n: sem(n) for n in names}
        toep_in = [sem(f"toep_in{i}") for i in range(SLOTS)]

        passed = {str(e.engine): sem(f"passed{i}") for i, e in enumerate((nc.scalar, nc.vector, nc.gpsimd))}

        block = ctx.enter_context(nc.Block())
        x_tok = x.rearrange("(t p) c -> p t c", p=P)
        out_tok = out.rearrange("(t p) c -> p t c", p=P)
        res3 = res[:, :].rearrange("p (t c) -> p t c", c=P)

        def hold(engine, name, value):
            engine.wait_ge(S[name], value)
            engine.sem_inc(passed[str(engine.engine)], 1)

        def tok(s, j):
            return res[:, ds(s * GT + j * P, P)]

        def group(s):
            return res[:, ds(s * GT, GT)]

        def by_channel(ap):
            return ap.rearrange("p (j g c) -> p g c j", j=TILES, c=CG)

        def packed(ap):
            return ap.rearrange("p (g c j) -> p g c j", j=TILES, c=CG)

        def xv_part(n, s):
            v = xv[:, :].rearrange("p (g q) -> p g q", q=REG)[:, :, n * CG * NT:(n + 1) * CG * NT]
            return v.rearrange("p g (c t) -> p g c t", t=NT)[:, :, :, ds(s * TILES, TILES)]

        def y_group(s):
            v = y_all.rearrange("p (g q) -> p g q", q=REG // 2)[:, :, 0:CG * NT]
            return v.rearrange("p g (c t) -> p g c t", t=NT)[:, :, :, ds(s * TILES, TILES)]

        def mod_rows(first, count, s):
            v = mod_dram.ap()[ds(s * SEQ, SEQ), first * P:(first + count) * P]
            return bass.AP(tensor=v.tensor, offset=v.offset, ap=[[0, P]] + [list(d) for d in v.ap])

        def mod_tile(t, row, rows, b):
            at = (b * rows + row) * P
            return t[:, at:at + P]

        P1_LAG = 3

        def phase1(engine, step):
            for s in range(P1_LAG):
                step(s)
            with engine.Fori(P1_LAG, NG) as s:
                step(s, True)
            for s in range(NG, NG + P1_LAG):
                step(s)

        def has(s, g_lag, loop):
            return loop or 0 <= s - g_lag < NG

        def phase3(engine, step):
            step(0, True, False)
            with engine.Fori(1, NG) as s:
                step(s, True, True)
            step(NG, False, True)

        KS = UP + 2 * FFC
        UB = bank[4:8]

        def up_filled(s, k):
            return s * KS - UP + k + 1

        def up_emptied(s, k):
            return s * (KS // 2) - UP // 2 + k // 2 + 1

        @block.sync
        def _(sp):
            sp.dma_start(cst[:, :], setup).then_inc(S["setup_in"], 16)
            sp.dma_start(res3[:, 0:P1_LAG * TILES, :], x_tok[:, 0:P1_LAG * TILES, :]).then_inc(S["x_in0"], 16)
            b2_all = bass.AP(tensor=b2.tensor, offset=0, ap=[[0, batch], [1, 3 * P]])
            sp.dma_start(bias2, b2_all).then_inc(S["bias2_in"], 16)
            sp.dma_start(win_sb[:, :], win).then_inc(S["win_in"], 16)
            sp.dma_start(res3[:, P1_LAG * TILES:, :], x_tok[:, P1_LAG * TILES:, :]).then_inc(S["x_in1"], 16)
            sp.dma_start(w_sb[:, :], weights).then_inc(S["w_in"], 16)
            sp.dma_start(l3_sb[:, :], l3w).then_inc(S["w_in"], 16)
            sp.wait_ge(S["mod_ready"], 1)
            sp.dma_start(mod_dram.ap(), mod_sb).then_inc(S["mod_out"], 16)
            sp.wait_ge(S["mod_out"], 16)
            sp.dma_start(mod1[:, :], mod_rows(0, 2, 0)).then_inc(S["mod1_in"], 16)
            sp.wait_ge(S["filt_ready"], 1)
            sp.dma_start(filt_dram.ap(), filt_p).then_inc(S["filt_out"], 16)
            sp.wait_ge(S["filt_out"], 16)

            def load_toeplitz(cg, slot):
                src = filt_dram.ap()[ds(cg * CG, CG), 0:1]
                rows = bass.AP(tensor=src.tensor, offset=src.offset, ap=[[1, P], [HW, CG * PARTS], [1, 2 * P]])
                dst = toep[:, slot * toep_w:(slot + 1) * toep_w].rearrange("p (r k) -> p r k", k=2 * P)
                sp.dma_start(dst, rows).then_inc(toep_in[slot], 16)

            for slot in range(SLOTS):
                load_toeplitz(slot, slot)

            def load_mod1(s):
                sp.wait_ge(S["h_s"], s)
                sp.dma_start(mod1[:, :], mod_rows(0, 2, s)).then_inc(S["mod1_in"], 16)

            with sp.Fori(1, NG) as s:
                load_mod1(s)

            with sp.Fori(1, NCG // SLOTS) as r:
                for slot in range(SLOTS):
                    sp.wait_ge(S["conv_mm"], (r - 1) * SLOTS + slot + 1)
                    load_toeplitz(r * SLOTS + slot, slot)

            sp.wait_ge(S["rest_free"], NG + 1)
            sp.dma_start(xin3, x_tok[:, 0:TILES, :]).then_inc(S["xin_in"], 16)
            sp.dma_start(mod3[:, :], mod_rows(2, 4, 0)).then_inc(S["mod3_in"], 16)

            def step(s, mixer, ffn, last=False):
                if mixer and not last:
                    sp.wait_ge(S["xn_s"], s + 1)
                    sp.dma_start(xin3, x_tok[:, ds((s + 1) * TILES, TILES), :]).then_inc(S["xin_in"], 16)
                    sp.wait_ge(S["addb"], s + 1)
                    sp.dma_start(mod3[:, :], mod_rows(2, 4, s + 1)).then_inc(S["mod3_in"], 16)
                if ffn:
                    sp.wait_ge(S["fin"], s)
                    sp.dma_start(out_tok[:, ds((s - 1) * TILES, TILES), :], res3[:, ds((s - 1) * TILES, TILES), :]).then_inc(S["stored"], 16)
                if mixer:
                    if ffn:
                        sp.wait_ge(S["down_free"], s + 1)
                    sp.dma_start(modg, mod_rows(6, 1, s)).then_inc(S["modg_in"], 16)

            step(0, True, False)
            with sp.Fori(1, NG - 1) as s:
                step(s, True, True)
            step(NG - 1, True, True, last=True)
            step(NG, False, True)
            sp.wait_ge(S["stored"], 16 * NG)

        @block.scalar
        def _(act):
            act.wait_ge(S["setup_in"], 16)
            act.activation(silu_c[:, :], C("cT"), ACT.Silu).then_inc(S["silu"], 1)
            for n in range(poles):
                if n >= 4:
                    act.wait_ge(S["filt_acc"], n - 3)
                lp = C("log_poles")[:, n:n + 1]
                act.activation(decay[n % 4], C("time"), ACT.Exp, scale=lp).then_inc(S["decay_done"], 1)

            def step(s, loop=False):
                if has(s, 1, loop):
                    hold(act, "h_s", s)
                    for j in range(TILES):
                        i = act.activation(junk[:, j * P:(j + 1) * P], tok(s - 1, j), ACT.Square, accum_out=sumsq1[:, j:j + 1])
                    i.then_inc(S["sumsq1_s"], 1)
                if has(s, 2, loop):
                    for n, (k, dst) in enumerate(((1, acc1[:, :]), (2, accv[:, :]), (0, x2T[:, ds((s - 2) * GT, GT)]))):
                        hold(act, "z_s", (s - 2) * 3 + n + 1)
                        if n < 2 and has(s, 3, loop):
                            hold(act, "xvT_s", s - 2)
                        act.activation(dst, bank[1 + n][:, :], ACT.Identity, scale=C("short_w")[:, 3 * k + 2:3 * k + 3],
                                       bias=C("short_b")[:, k:k + 1]).then_inc(S["acc_s"], 1)
                if has(s, 1, loop):
                    hold(act, "rms1_s", s)
                    if has(s, 2, loop):
                        hold(act, "trh", s - 1)
                    for j in range(TILES):
                        i = act.activation(hnorm[:, j * P:(j + 1) * P], tok(s - 1, j), ACT.Copy, scale=rms1[:, j:j + 1])
                    i.then_inc(S["hnorm_s"], 1)
                    act.wait_ge(S["trh"], s)
                    if has(s, 2, loop):
                        act.wait_ge(S["z_s"], (s - 1) * 3)
                    act.activation(hT[:, :], bank[0][:, :], ACT.Copy).then_inc(S["hT_s"], 1)
                if has(s, 3, loop):
                    hold(act, "trx", s - 2)
                    act.activation(xv_part(0, s - 3), by_channel(bank[4][:, :]), ACT.Copy).then_inc(S["xv1_s"], 1)

            phase1(act, step)

            def put(cg, b):
                hold(act, "conv_mm", cg + 1)
                act.activation(y_all[:, ds(cg * (REG // 2), CG * NT)], bank[4 + b][:, :], ACT.Copy).then_inc(S["y_act"], 1)

            act.sem_inc(S["y_act"], 1)
            with act.Fori(0, NCG // SLOTS) as r:
                for b in range(0, SLOTS, 2):
                    put(r * SLOTS + b, b)

            def relu(s, k):
                act.wait_ge(S["up_mm"], up_filled(s, k))
                act.activation(hid[:, k * GT:(k + 1) * GT], UB[k % 4][:, :], ACT.Relu,
                               bias=W("up_b")[:, k:k + 1]).then_inc(S["up_act"], 1)

            def step3(s, mixer, ffn):
                if ffn:
                    for k in (0, 2, 4):
                        relu(s, k)
                if mixer:
                    act.wait_ge(S["y2_s"], s + 1)
                    for j in range(TILES):
                        i = act.activation(junk[:, j * P:(j + 1) * P], y2[:, j * P:(j + 1) * P], ACT.Square, accum_out=sumsq1[:, j:j + 1])
                    i.then_inc(S["sumsq2"], 1)
                if ffn:
                    relu(s, 6)
                if mixer:
                    act.wait_ge(S["rms2"], s + 1)
                    for j in range(TILES):
                        i = act.activation(znorm[:, j * P:(j + 1) * P], y2[:, j * P:(j + 1) * P], ACT.Copy, scale=rms1[:, j:j + 1])
                    i.then_inc(S["znorm_s"], 1)
                if ffn:
                    relu(s, 8)
                if mixer:
                    act.wait_ge(S["trZ"], s + 1)
                    act.activation(zT, bank[1][:, :], ACT.Copy).then_inc(S["zT_s"], 1)
                if ffn:
                    relu(s, 10)
                if mixer:
                    for n in range(FFC):
                        k = UP + 2 * n
                        act.wait_ge(S["up_mm"], up_filled(s, k))
                        act.activation(mlp[:, n * GT:(n + 1) * GT], UB[k % 4][0:FW, :], ACT.Gelu_apprx_tanh).then_inc(S["up_act"], 1)
                    act.wait_ge(S["trH"], s + 1)
                    act.activation(h2T[:, :], bank[0][:, :], ACT.Copy).then_inc(S["h2T_s"], 1)

            phase3(act, step3)

        @block.vector
        def _(dve):
            dve.wait_ge(S["setup_in"], 16)
            dve.wait_ge(S["mod_mm"], 1)
            m = bank[5][0:batch, :]
            m2 = bank[6][0:batch, 0:2 * P]

            def row(n, count=1):
                return mod_sb[:, n * P:(n + count) * P]

            dve.wait_ge(S["bias2_in"], 16)
            dve.tensor_scalar(row(0), m[:, P:2 * P], 1.0, None, ALU.add)
            dve.tensor_copy(row(1), m[:, 0:P])
            dve.tensor_scalar(row(3), m2[:, 0:P], 1.0, None, ALU.add)
            dve.tensor_copy(row(4), m[:, 3 * P:4 * P])
            dve.tensor_scalar(sign[:, 0:P], m[:, 2 * P:3 * P], 0.0, 2.0, ALU.is_ge, ALU.mult)
            dve.tensor_scalar(sign[:, P:2 * P], m2[:, P:2 * P], 0.0, 2.0, ALU.is_ge, ALU.mult)
            dve.tensor_copy(row(2), m[:, 2 * P:3 * P])
            dve.tensor_copy(row(6), m2[:, P:2 * P])
            dve.tensor_tensor(bias2[:, 0:P], bias2[:, 0:P], bias2[:, P:2 * P], ALU.add).then_inc(S["mod_a"], 1)
            dve.wait_ge(S["mod_a"], 1)
            dve.tensor_tensor(bias2[:, 0:P], bias2[:, 0:P], bias2[:, 2 * P:3 * P], ALU.add)
            dve.tensor_scalar(sign, sign, -1.0, None, ALU.add)
            for n in (2, 6):
                i = dve.scalar_tensor_tensor(row(n), row(n), -1.0, row(n), ALU.mult, ALU.max)
            i.then_inc(S["mod_b"], 1)
            dve.wait_ge(S["mod_b"], 1)
            for n, at_s in ((2, 0), (6, P)):
                i = dve.scalar_tensor_tensor(row(n), row(n), 0.25, sign[:, at_s:at_s + P], ALU.max, ALU.mult)
            i.then_inc(S["mod_c"], 1)
            dve.wait_ge(S["mod_c"], 1)
            dve.tensor_tensor(row(5), row(6), bias2[:, 0:P], ALU.mult).then_inc(S["mod_ready"], 1)

            for n in range(poles):
                dve.wait_ge(S["decay_done"], n + 1)
                r = C("residues")[:, n:n + 1]
                if n == 0:
                    dve.tensor_scalar(filt, decay[0], r, None, ALU.mult).then_inc(S["filt_acc"], 1)
                else:
                    dve.wait_ge(S["filt_acc"], n)
                    dve.scalar_tensor_tensor(filt, decay[n % 4], r, filt, ALU.mult, ALU.add).then_inc(S["filt_acc"], 1)
            dve.memset(filt_p, 0.0).then_inc(S["filt_d"], 1)
            dve.wait_ge(S["filt_acc"], poles)
            dve.tensor_tensor(filt[:, 0:1], filt[:, 0:1], C("d_skip"), ALU.add).then_inc(S["filt_d"], 1)
            dve.wait_ge(S["filt_d"], 2)
            taps = [filt_p[:, n * HW + P - 1:n * HW + P - 1 + length] for n in range(PARTS)]
            dve.tensor_copy(taps[0], filt).then_inc(S["filt_1"], 1)
            dve.wait_ge(S["filt_1"], 1)
            dve.tensor_tensor(filt_r[0], filt, taps[0], ALU.subtract).then_inc(S["filt_2"], 1)
            dve.wait_ge(S["filt_2"], 1)
            dve.tensor_copy(taps[1], filt_r[0]).then_inc(S["filt_3"], 1)
            dve.wait_ge(S["filt_3"], 1)
            dve.tensor_tensor(taps[2], filt_r[0], taps[1], ALU.subtract).then_inc(S["filt_ready"], 1)
            dve.wait_ge(S["win_in"], 16)
            dve.tensor_scalar(win_sb[:, :], win_sb[:, :], C("pre_w"), None, ALU.mult).then_inc(S["win_scaled"], 1)
            dve.tensor_tensor(small[:, 0:1], C("gate")[:, 1:2], C("gate")[:, 0:1], ALU.subtract).then_inc(S["gate_set"], 1)
            dve.wait_ge(S["w_in"], 32)
            l12 = w_sb[:, wc["l1"][0]:wc["l2"][1]]
            dve.tensor_scalar(l12, l12, C("post_w"), None, ALU.mult).then_inc(S["w_scaled"], 1)
            dve.wait_ge(S["gate_set"], 1)
            dve.tensor_scalar(gate_sb[:, :], C("time")[:, 0:P], 0.0, small[:, 0:1], ALU.mult, ALU.add).then_inc(S["gate_set"], 1)
            dve.wait_ge(S["mod_out"], 16)
            dve.wait_ge(S["filt_out"], 16)

            def normalise(s, veps, dst, mean, rstd, rows, scale_row, shift_row, tag):
                for j in range(TILES):
                    i = dve.scalar_tensor_tensor(cent[:, j * P:(j + 1) * P], tok(s, j), mean[:, 2 * j:2 * j + 1],
                                                 mod_tile(rows, scale_row[0], scale_row[1], j * P // length),
                                                 ALU.subtract, ALU.mult)
                i.then_inc(S[tag], 1)
                dve.wait_ge(S[tag], s + 1)
                for j in range(TILES):
                    i = dve.scalar_tensor_tensor(dst(j), cent[:, j * P:(j + 1) * P], rstd[:, j:j + 1],
                                                 mod_tile(rows, shift_row[0], shift_row[1], j * P // length),
                                                 ALU.mult, ALU.add)
                return i

            def statistics(s, bn, mvar):
                for j in range(TILES):
                    i = dve.bn_stats(stats1[:, 6 * j:6 * j + 6], tok(s, j))
                i.then_inc(S[bn], 1)
                hold(dve, bn, s + 1)
                for j in range(TILES):
                    i = dve.bn_aggr(mv1[:, 2 * j:2 * j + 2], stats1[:, 6 * j:6 * j + 6])
                i.then_inc(S[mvar], 1)

            def step(s, loop=False):
                if has(s, 0, loop):
                    dve.wait_ge(S["x_in0"], 16)
                    if loop:
                        dve.wait_ge(S["x_in1"], 16)
                    statistics(s, "bn1", "mvar1")
                if has(s, 3, loop):
                    dve.wait_ge(S["xv1_s"], s - 2)
                    dve.wait_ge(S["rest_free"], s - 2)
                    dve.tensor_tensor(packed(rest[:, :]), by_channel(bank[4][:, :]), xv_part(0, s - 3),
                                      ALU.subtract).then_inc(S["rest_s"], 1)
                if has(s, 2, loop):
                    def tap(n, lag):
                        k = (1, 2, 0)[n]
                        dst = (acc1[:, :], accv[:, :], x2T[:, ds((s - 2) * GT, GT)])[n]
                        v = dst.rearrange("p (b t) -> p b t", t=length)[:, :, lag:length]
                        z = bank[1 + n][:, :].rearrange("p (b t) -> p b t", t=length)[:, :, 0:length - lag]
                        return dve.scalar_tensor_tensor(v, z, C("short_w")[:, 3 * k + 2 - lag:3 * k + 3 - lag], v,
                                                        ALU.mult, ALU.add)
                    for n in range(3):
                        dve.wait_ge(S["acc_s"], (s - 2) * 3 + n + 1)
                        tap(n, 1).then_inc(S["tap1"], 1)
                        if n == 1 or n == 2:
                            m = 0 if n == 1 else 1
                            dve.wait_ge(S["tap1"], (s - 2) * 3 + m + 1)
                            tap(m, 2).then_inc(S["conv_s"], 1)
                    dve.wait_ge(S["tap1"], (s - 2) * 3 + 3)
                    tap(2, 2).then_inc(S["conv_s"], 1)
                if has(s, 0, loop):
                    dve.wait_ge(S["rstd1_s"], s + 1)
                    dve.wait_ge(S["mod1_in"], (s + 1) * 16)
                    normalise(s, None, lambda j: tok(s, j), mv1, rstd1, mod1, (0, 2), (1, 2), "cent_s").then_inc(S["h_s"], 1)

            phase1(dve, step)

            def put(cg, b):
                dve.wait_ge(S["conv_mm"], cg + 1)
                dve.tensor_copy(y_all[:, ds(cg * (REG // 2), CG * NT)], bank[4 + b][:, :]).then_inc(S["y_dve"], 1)

            dve.sem_inc(S["y_dve"], 1)
            with dve.Fori(0, NCG // SLOTS) as r:
                for b in range(1, SLOTS, 2):
                    put(r * SLOTS + b, b)

            def relu(s, k):
                dve.wait_ge(S["up_mm"], up_filled(s, k))
                dve.tensor_scalar(hid[:, k * GT:(k + 1) * GT], UB[k % 4][:, :], W("up_b")[:, k:k + 1], 0.0,
                                  ALU.add, ALU.max).then_inc(S["up_dve"], 1)

            def per_sequence(t, row, rows):
                v = t[:, :].rearrange("p (b r c) -> p b r c", b=SEQ, r=rows)[:, :, row:row + 1, :]
                return v.to_broadcast([P, SEQ, TILES // SEQ, P])

            def tiles(ap):
                return ap.rearrange("p (b q c) -> p b q c", b=SEQ, c=P)

            def step3(s, mixer, ffn):
                if mixer:
                    dve.wait_ge(S["trY"], s + 1)
                    dve.tensor_tensor(yx, bank[0][:, :], x2T[:, ds(s * GT, GT)], ALU.mult).then_inc(S["yx_s"], 1)
                if ffn:
                    for k in (1, 3):
                        relu(s, k)
                if mixer:
                    dve.wait_ge(S["outp"], s + 1)
                    dve.tensor_tensor(y2, bank[2][:, :], group(s), ALU.add).then_inc(S["y2_s"], 1)
                if ffn:
                    for k in (5, 7, 9, 11):
                        relu(s, k)
                if mixer:
                    for n in range(FFC):
                        k = UP + 2 * n + 1
                        dve.wait_ge(S["up_mm"], up_filled(s, k))
                        dve.wait_ge(S["up_act"], up_emptied(s, k - 1))
                        m = mlp[:, n * GT:(n + 1) * GT]
                        dve.tensor_tensor(m, UB[k % 4][0:FW, :], m, ALU.mult).then_inc(S["up_dve"], 1)
                    dve.wait_ge(S["l3_mm"], s + 1)
                    dve.tensor_tensor(y2, bank[2][:, :], y2, ALU.add).then_inc(S["a_s"], 1)
                    dve.wait_ge(S["a_s"], s + 1)
                    dve.wait_ge(S["mod3_in"], (s + 1) * 16)
                    dve.tensor_tensor(tiles(y2), tiles(y2), per_sequence(mod3, 0, 4), ALU.mult).then_inc(S["ag_s"], 1)
                    dve.wait_ge(S["ag_s"], s + 1)
                    dve.wait_ge(S["xin_in"], (s + 1) * 16)
                    dve.tensor_tensor(group(s), y2, xin, ALU.add).then_inc(S["xn_s"], 1)
                    hold(dve, "xn_s", s + 1)
                    statistics(s, "bn2", "mvar2")
                    dve.wait_ge(S["rstd2_s"], s + 1)
                    normalise(s, None, lambda j: hn2[:, j * P:(j + 1) * P], mv1, rstd1, mod3, (1, 4), (2, 4), "cent2").then_inc(S["h2_s"], 1)
                if ffn:
                    dve.wait_ge(S["down_mm"], s)
                    dve.wait_ge(S["modg_in"], s * 16)
                    v = modg.rearrange("p (b r c) -> p b r c", b=SEQ, r=1).to_broadcast([P, SEQ, TILES // SEQ, P])
                    dve.tensor_tensor(tiles(ffo2), tiles(bank[3][:, :]), v, ALU.mult).then_inc(S["down_free"], 1)
                if mixer:
                    dve.wait_ge(S["router"], s + 1)
                    dve.scalar_tensor_tensor(h2T1[:, :], bank[1][:, :], 0.0, h2T[:, :], ALU.is_gt, ALU.mult).then_inc(S["x1_s"], 1)

            dve.sem_inc(S["down_free"], 1)
            phase3(dve, step3)

        @block.gpsimd
        def _(pool):
            pool.sem_inc(S["rest_free"], 1)
            pool.memset(half[:, :], -0.5).then_inc(S["half_set"], 1)
            pool.wait_ge(S["half_set"], 1)
            pool.wait_ge(S["mod_out"], 16)

            def inverse_root(dst, src, mul, eps, mid, done, n):
                pool.tensor_scalar(dst, src, mul, eps, ALU.mult, ALU.add).then_inc(S[mid], 1)
                pool.wait_ge(S[mid], n)
                pool.tensor_tensor(dst, dst, half[:, :], ALU.pow).then_inc(S[done], 1)

            var = mv1[:, :].rearrange("p (j k) -> p j k", k=2)[:, :, 1]

            def step(s, loop=False):
                if has(s, 0, loop):
                    hold(pool, "mvar1", s + 1)
                    if has(s, 1, loop):
                        hold(pool, "h_s", s)
                    inverse_root(rstd1[:, :], var, 1.0, LN_EPS, "veps1", "rstd1_s", s + 1)
                if has(s, 1, loop):
                    hold(pool, "sumsq1_s", s)
                    if has(s, 2, loop):
                        hold(pool, "hnorm_s", s - 1)
                    inverse_root(rms1[:, :], sumsq1[:, :], 1.0 / P, RMS_EPS, "meps1", "rms1_s", s)
                if has(s, 2, loop):
                    pool.wait_ge(S["conv_s"], (s - 2) * 3 + 2)
                    if has(s, 3, loop):
                        pool.wait_ge(S["trx"], s - 2)
                    a, v, dst = (t[:, :].rearrange("p (j t) -> p j t", t=P) for t in (acc1, accv, xvT))
                    pool.tensor_tensor(dst[:, :, ::-1], a, v, ALU.mult).then_inc(S["xvT_s"], 1)
                if has(s, 3, loop):
                    pool.wait_ge(S["rest_s"], s - 2)
                    pool.tensor_copy(xv_part(1, s - 3), packed(rest[:, :])).then_inc(S["xv2_s"], 1)
                    pool.wait_ge(S["xv2_s"], s - 2)
                    pool.tensor_tensor(xv_part(2, s - 3), packed(rest[:, :]), xv_part(1, s - 3), ALU.subtract).then_inc(S["rest_free"], 1)

            phase1(pool, step)

            def copy_y(s):
                pool.tensor_copy(by_channel(yc[:, :]), y_group(s)).then_inc(S["yc_s"], 1)

            pool.wait_ge(S["y_act"], NCG // 2 + 1)
            pool.wait_ge(S["y_dve"], NCG // 2 + 1)
            copy_y(0)

            def step3(s, mixer, ffn, last=False):
                if mixer:
                    hold(pool, "sumsq2", s + 1)
                    inverse_root(rms1[:, :], sumsq1[:, :], 1.0 / P, RMS_EPS, "meps2", "rms2", s + 1)
                    if not last:
                        pool.wait_ge(S["trY"], s + 1)
                        copy_y(s + 1)
                    hold(pool, "mvar2", s + 1)
                    inverse_root(rstd1[:, :], var, 1.0, LN_EPS, "veps2", "rstd2_s", s + 1)
                    pool.wait_ge(S["h2_s"], s + 1)
                    for j in range(TILES):
                        i = pool.tensor_tensor(tok(s, j), tok(s, j), mod_tile(mod3, 3, 4, j * P // length), ALU.add)
                    i.then_inc(S["addb"], 1)
                if ffn:
                    pool.wait_ge(S["down_free"], s + 1)
                    pool.wait_ge(S["addb"], s)
                    pool.tensor_tensor(group(s - 1), group(s - 1), ffo2, ALU.add).then_inc(S["fin"], 1)
                if mixer:
                    pool.wait_ge(S["x1_s"], s + 1)
                    pool.tensor_tensor(h2T0[:, :], h2T[:, :], h2T1[:, :], ALU.subtract).then_inc(S["x0_s"], 1)

            step3(0, True, False)
            with pool.Fori(1, NG - 1) as s:
                step3(s, True, True)
            step3(NG - 1, True, True, last=True)
            step3(NG, False, True)

        @block.tensor
        def _(pe):
            pe.wait_ge(S["silu"], 1)
            pe.matmul(bank[5][0:batch, :], silu_c[:, :], C("wmod")[:, 0:512], start=True, stop=True)
            pe.matmul(bank[6][0:batch, 0:256], silu_c[:, :], C("wmod")[:, 512:768], start=True, stop=True).then_inc(S["mod_mm"], 1)
            pe.wait_ge(S["win_scaled"], 1)

            def transposes(dst, src):
                for j in range(TILES):
                    i = pe.transpose(dst[:, j * P:(j + 1) * P], src[:, j * P:(j + 1) * P], ident)
                return i

            def step(s, loop=False):
                if has(s, 1, loop):
                    pe.wait_ge(S["hnorm_s"], s)
                    if has(s, 2, loop):
                        pe.wait_ge(S["hT_s"], s - 1)
                    transposes(bank[0], hnorm).then_inc(S["trh"], 1)
                    pe.wait_ge(S["hT_s"], s)
                    for n, k in enumerate((1, 2, 0)):
                        if has(s, 2, loop):
                            pe.wait_ge(S["conv_s"], (s - 2) * 3 + n + 1)
                        pe.matmul(bank[1 + n][:, :], win_sb[:, k * P:(k + 1) * P], hT[:, :], start=True, stop=True).then_inc(S["z_s"], 1)
                if has(s, 2, loop):
                    pe.wait_ge(S["xvT_s"], s - 1)
                    if has(s, 3, loop):
                        pe.wait_ge(S["rest_s"], s - 2)
                    transposes(bank[4], xvT).then_inc(S["trx"], 1)

            phase1(pe, step)

            pe.wait_ge(S["rest_free"], NG + 1)
            with pe.Fori(0, NCG // SLOTS) as r:
                for slot in range(SLOTS):
                    pe.wait_ge(toep_in[slot], (r + 1) * 16)
                    if slot % 2 == 0:
                        pe.wait_ge(S["y_act"], r * 2 + slot // 2 + 1)
                    else:
                        pe.wait_ge(S["y_dve"], r * 2 + slot // 2 + 1)
                    dst = bank[4 + slot][:, :].rearrange("p (c b h) -> p c b h", c=CG, h=2)
                    for c in range(CG):
                        T = toep[:, slot * toep_w + c * PARTS * 2 * P:slot * toep_w + (c + 1) * PARTS * 2 * P]
                        first = True
                        for part_t in range(PARTS):
                            for part_x in range(PARTS - part_t):
                                at_x = (r * SLOTS + slot) * REG + part_x * CG * NT + c * NT
                                last = part_t == PARTS - 1
                                rows = xv[:, ds(at_x, NT)].rearrange("p (b h) -> p b h", h=2)
                                t0 = part_t * 2 * P
                                pe.matmul(dst[:, c, :, :], T[:, t0:t0 + P], rows, start=first, stop=False,
                                          skip_group_check=True)
                                i = pe.matmul(dst[:, c, :, 1], T[:, t0 + P:t0 + 2 * P], rows[:, :, 0], start=False,
                                              stop=last, skip_group_check=True)
                                first = False
                    i.then_inc(S["conv_mm"], 1)

            pe.wait_ge(S["w_scaled"], 1)
            pe.wait_ge(S["gate_set"], 2)

            def up_free(s, k):
                before = (s, k - 4) if k >= 4 else (s - 1, KS - 2 + k if k < 2 else KS - 6 + k)
                if isinstance(s, int) and s == 0 and k - 4 < UP:
                    return
                pe.wait_ge(S["up_act" if k % 2 == 0 else "up_dve"], up_emptied(*before))

            def up(s, k, src):
                up_free(s, k)
                pe.matmul(UB[k % 4][:, :], W("up")[:, k * P:(k + 1) * P], src, start=True, stop=True).then_inc(S["up_mm"], 1)

            def down(tile, done):
                for n in range(UP):
                    i = pe.matmul(bank[3][:, tile * P:(tile + 1) * P], hid[:, n * GT + tile * P:n * GT + (tile + 1) * P],
                                  W("down")[:, n * P:(n + 1) * P], start=n == 0, stop=n == UP - 1)
                if done:
                    i.then_inc(S["down_mm"], 1)

            def step3(s, mixer, ffn):
                if mixer:
                    pe.wait_ge(S["yc_s"], s + 1)
                    if ffn:
                        pe.wait_ge(S["h2T_s"], s)
                    transposes(bank[0], yc).then_inc(S["trY"], 1)
                if ffn:
                    for k in range(0, 4):
                        up(s, k, h2T[:, :])
                if mixer:
                    pe.wait_ge(S["yx_s"], s + 1)
                    if ffn:
                        pe.wait_ge(S["a_s"], s)
                    for j in range(TILES):
                        i = pe.matmul(bank[2][:, j * P:(j + 1) * P], yx[:, j * P:(j + 1) * P], W("out"), start=True, stop=True)
                    i.then_inc(S["outp"], 1)
                if ffn:
                    pe.wait_ge(S["x1_s"], s)
                    for k in range(4, 8):
                        up(s, k, h2T1[:, :])
                if mixer:
                    pe.wait_ge(S["znorm_s"], s + 1)
                    transposes(bank[1], znorm).then_inc(S["trZ"], 1)
                if ffn:
                    pe.wait_ge(S["x0_s"], s)
                    for k in range(8, 12):
                        up(s, k, h2T0[:, :])
                if mixer:
                    pe.wait_ge(S["zT_s"], s + 1)
                    for k in range(UP, KS):
                        n, second = (k - UP) // 2, (k - UP) % 2
                        w = W("l2" if second else "l1")
                        up_free(s, k)
                        pe.matmul(UB[k % 4][0:FW, :], w[:, n * FW:(n + 1) * FW], zT, start=True, stop=True).then_inc(S["up_mm"], 1)
                if ffn:
                    pe.wait_ge(S["up_act"], up_emptied(s, UP - 2))
                    pe.wait_ge(S["up_dve"], up_emptied(s, UP - 1))
                    pe.wait_ge(S["down_free"], s)
                    down(0, False)
                if mixer:
                    pe.wait_ge(S["up_dve"], up_emptied(s, KS - 1))
                    pe.wait_ge(S["y2_s"], s + 1)
                    for j in range(TILES):
                        for n in range(FFC):
                            i = pe.matmul(bank[2][:, j * P:(j + 1) * P], mlp[:, n * GT + j * P:n * GT + (j + 1) * P],
                                          l3_sb[:, n * P:(n + 1) * P], start=n == 0, stop=n == FFC - 1)
                    i.then_inc(S["l3_mm"], 1)
                if ffn:
                    down(1, False)
                    down(2, False)
                if mixer:
                    pe.wait_ge(S["h2_s"], s + 1)
                    pe.wait_ge(S["yx_s"], s + 1)
                    transposes(bank[0], hn2).then_inc(S["trH"], 1)
                if ffn:
                    down(3, True)
                if mixer:
                    pe.wait_ge(S["h2T_s"], s + 1)
                    pe.matmul(bank[1][:, :], gate_sb[:, :], h2T[:, :], start=True, stop=True).then_inc(S["router"], 1)

            phase3(pe, step3)


def kernel(**inputs):
    import numpy as np
    import concourse.bacc as bacc
    from concourse.bass_utils import run_bass_kernel_spmd

    a = {k.removeprefix("L0_"): np.asarray(v) for k, v in inputs.items()}
    u = a["attn_u"]
    batch, length, d = u.shape
    poles, ff, hidden = a["attn_residues"].shape[1], a["attn_l1_w"].shape[0], a["ffn_sw1"].shape[1]
    f = np.float32

    def chunks(w, rows):
        return w.reshape(-1, rows, w.shape[-1]).transpose(1, 0, 2).reshape(rows, -1)

    setup = np.concatenate([
        a["c"].T, a["wmod"], a["attn_residues"], a["attn_log_poles"][:, :, 0], a["attn_D_skip"][:, None],
        chunks(a["attn_short_w"][:, 0, :], d), a["attn_short_b"].reshape(3, d).T, a["attn_pre_norm_w"][:, None],
        a["attn_post_norm_w"][:, None], a["ffn_gate_w"].T, np.eye(d, dtype=f),
        np.broadcast_to(np.arange(length, dtype=f), (d, length))], axis=1)
    ups = [a["ffn_sw1"], a["ffn_w1"][1], a["ffn_w1"][0]]
    downs = [a["ffn_sw2"], a["ffn_w2"][1], a["ffn_w2"][0]]
    up_b = [a["ffn_sb1"], a["ffn_b1"][1], a["ffn_b1"][0]]
    weights = np.concatenate([a["attn_out_proj_w"].T, a["attn_l1_w"].T, a["attn_l2_w"].T] + ups
                             + [chunks(w, P) for w in downs] + [b.reshape(-1, P).T for b in up_b], axis=1)
    arrays = {
        "x": u.reshape(batch * length, d), "setup": setup, "win": a["attn_in_proj_w"].T, "weights": weights,
        "l3w": chunks(a["attn_l3_w"].T, ff // 3), "b2": np.concatenate([a["ffn_b2"].reshape(-1), a["ffn_sb2"]]),
    }
    arrays = {k: np.ascontiguousarray(v) for k, v in arrays.items()}
    nc = bacc.Bacc("TRN2", target_bir_lowering=False, num_devices=1)
    aps = {k: nc.dram_tensor(k, v.shape, mybir.dt.from_np(v.dtype), kind="ExternalInput").ap() for k, v in arrays.items()}
    out = nc.dram_tensor("out", (batch * length, d), F32, kind="ExternalOutput").ap()
    adaln_block(nc, aps["x"], aps["setup"], aps["win"], aps["weights"], aps["l3w"], aps["b2"], out,
                batch, length, poles, ff, hidden)
    r = run_bass_kernel_spmd(nc, [arrays], core_ids=[0])
    return r.results[0]["out"].reshape(batch, length, d)
```

```python
from contextlib import ExitStack

import concourse.bass as bass
from concourse import mybir

F32 = mybir.dt.float32
F32R = mybir.dt.float32r
BF16 = mybir.dt.bfloat16
ALU = mybir.AluOpType
ACT = mybir.ActivationFunctionType
ds = bass.ds

P = 128
LN_EPS = 1e-5
RMS_EPS = 1e-6
TILES = 4
GT = TILES * P


def pack_columns(widths):
    at, out = 0, {}
    for name, w in widths:
        out[name] = (at, at + w)
        at += w
    return out, at


def setup_columns(batch, poles, length):
    return pack_columns([("cT", batch), ("residues", poles), ("log_poles", poles), ("d_skip", 1),
                         ("short_w", 9), ("short_b", 3), ("pre_w", 1), ("post_w", 1), ("gate", 2),
                         ("ident", P), ("time", length)])


def weight_columns(hidden):
    return pack_columns([("out", P), ("down", 3 * hidden), ("up_b", 3 * hidden // P)])


def split_columns(ff, hidden):
    return pack_columns([("l1", ff), ("l2", ff), ("up", 3 * hidden), ("gate", P)])


def adaln_block(nc, x, setup, wmod, win, weights, raw, l3w, rows, out, batch, length, poles, ff, hidden):
    TOK = batch * length
    NG = TOK // GT
    NT = TOK // P
    SEQ = GT // length
    FFC = 3
    FW = ff // FFC
    UP = 3 * hidden // P
    CG = 8
    NCG = P // CG
    PARTS = 3
    REG = PARTS * CG * NT
    HW = 3 * P
    SLOTS = 4
    assert length == 2 * P and ff % FFC == 0 and FW <= P and NCG % SLOTS == 0
    sc, setup_w = setup_columns(batch, poles, length)
    wc, weights_w = weight_columns(hidden)
    fc, split_w = split_columns(ff, hidden)
    raw_w = split_w - P
    MOD = 7

    with ExitStack() as ctx:
        def sb(name, shape, dt=F32):
            return ctx.enter_context(nc.sbuf_tensor(name, shape, dt))

        def sem(name):
            return ctx.enter_context(nc.semaphore(name))

        bank = [ctx.enter_context(nc.psum_tensor(f"bank{i}", [P, 512], F32)) for i in range(8)]
        filt_dram = nc.dram_tensor("filter_parts", [P, PARTS * HW], BF16)
        mod_dram = nc.dram_tensor("modulation", [batch, MOD * P], F32)

        cst = sb("cst", [P, setup_w])
        w_sb = sb("w_sb", [P, weights_w])
        l3_sb = sb("l3_sb", [FW, FFC * P])
        w_hi = sb("w_hi", [P, split_w], F32R)
        w_lo = sb("w_lo", [P, split_w], F32R)
        res = sb("res", [P, TOK])
        x2T = sb("x2T", [P, TOK])
        xv = sb("xv", [P, NCG * REG], BF16)
        y_all = xv[:, :].bitcast(F32)
        toep_w = CG * PARTS * 2 * P
        stats = sb("stats", [P, TILES * 6])
        mv = sb("mv", [P, TILES * 2])
        rstd = sb("rstd", [P, TILES])
        sumsq = sb("sumsq", [P, TILES])
        rms = sb("rms", [P, TILES])
        half = sb("half", [P, TILES])
        gate_diff = sb("gate_diff", [P, 1])

        with ExitStack() as early:
            def sb1(name, width, dt=F32):
                return early.enter_context(nc.sbuf_tensor(name, [P, width], dt))

            toep = sb1("toep", SLOTS * toep_w, BF16)
            win_sb = sb1("win_sb", 3 * P)
            win_taps = sb1("win_taps", 3 * P)
            silu_c = sb1("silu_c", batch)
            mod1 = sb1("mod1", SEQ * 2 * P)
            cent1, hnorm, hT, acc1, accv, xvT, rest = (sb1(n, GT) for n in ("cent1", "hnorm", "hT", "acc1", "accv", "xvT", "rest"))
        hid = sb("hid", [P, UP * GT])
        mlp = sb("mlp", [FW, FFC * GT])
        yx, y2, yc, xin, ffo, cent2 = (sb(n, [P, GT]) for n in ("yx", "y2", "yc", "xin", "ffo", "cent2"))
        znorm = hn2 = yx
        zT, h2T, h2T1, h2T0 = ([sb(f"{n}_{h}", [P, GT], F32R) for h in ("hi", "lo")] for n in ("zT", "h2T", "h2T1", "h2T0"))
        mod3 = sb("mod3", [P, SEQ * 4 * P])
        modg = sb("modg", [P, SEQ * P])
        junk2 = sb("junk2", [P, GT], BF16)

        def C(name):
            return cst[:, sc[name][0]:sc[name][1]]

        def W(name):
            return w_sb[:, wc[name][0]:wc[name][1]]

        ident = C("ident")

        decay = [y_all[:, i * length:(i + 1) * length] for i in range(4)]
        filt = y_all[:, 4 * length:5 * length]
        filt_r = y_all[:, 5 * length:6 * length]
        filt_p = xv[:, 14 * length:14 * length + PARTS * HW]
        mod_at = 16 * length
        mod_sb = y_all[0:batch, mod_at:mod_at + MOD * P]
        bias2 = y_all[0:batch, mod_at + MOD * P:mod_at + (MOD + 3) * P]
        sign = y_all[0:batch, mod_at + (MOD + 3) * P:mod_at + (MOD + 5) * P]
        taps_row = y_all[:, mod_at + (MOD + 5) * P:mod_at + (MOD + 8) * P]
        raw_sb = x2T[:, TOK - raw_w:TOK]
        wmod_sb = x2T[:, TOK - raw_w - 6 * P:TOK - raw_w]

        names = """setup_in wmod_in win_in raw_in w_in x_in0 x_in1 rows_in mod_out filt_out silu mod_mm mod_a mod_b mod_c mod_ready
        half_set decay_done filt_acc filt_d filt_1 filt_2 filt_3 filt_ready win_scaled w_hi_s w_lo_s gate_set
        mod1_in bn1 mvar1 veps1 rstd1_s cent_s h_s sumsq1_s meps1 rms1_s hnorm_s trh hT_s z_s zx2_s acc_s x2_s tap1 conv_s
        xvT_s trx xv1_s rest_s xv2_s rest_free
        conv_mm y_act y_dve
        yc_s trY yx_s up_mm up_act up_dve outp y2_s sumsq2 meps2 rms2 znorm_s trZ zT_hi zT_lo l3_mm a_s ag_s xn_s
        bn2 mvar2 veps2 rstd2_s cent2_s h2_s trH h2T_hi h2T_lo router x1_s x0_s down_mm down_free addb fin
        xin_in mod3_in modg_in stored""".split()
        S = {n: sem(n) for n in names}
        toep_in = [sem(f"toep_in{i}") for i in range(SLOTS)]

        passed = {str(e.engine): sem(f"passed{i}") for i, e in enumerate((nc.scalar, nc.vector, nc.gpsimd))}

        block = ctx.enter_context(nc.Block())
        x_tok = x.rearrange("(t p) c -> p t c", p=P)
        xin3 = xin[:, :].rearrange("p (t c) -> p t c", c=P)
        out_tok = out.rearrange("(t p) c -> p t c", p=P)
        res3 = res[:, :].rearrange("p (t c) -> p t c", c=P)

        def hold(engine, name, value):
            engine.wait_ge(S[name], value)
            engine.sem_inc(passed[str(engine.engine)], 1)

        def tok(s, j):
            return res[:, ds(s * GT + j * P, P)]

        def group(s):
            return res[:, ds(s * GT, GT)]

        def by_channel(ap):
            return ap.rearrange("p (j g c) -> p g c j", j=TILES, c=CG)

        def packed(ap):
            return ap.rearrange("p (g c j) -> p g c j", j=TILES, c=CG)

        def xv_part(n, s):
            v = xv[:, :].rearrange("p (g q) -> p g q", q=REG)[:, :, n * CG * NT:(n + 1) * CG * NT]
            return v.rearrange("p g (c t) -> p g c t", t=NT)[:, :, :, ds(s * TILES, TILES)]

        def y_group(s):
            v = y_all.rearrange("p (g q) -> p g q", q=REG // 2)[:, :, 0:CG * NT]
            return v.rearrange("p g (c t) -> p g c t", t=NT)[:, :, :, ds(s * TILES, TILES)]

        def mod_rows(first, count, s):
            v = mod_dram.ap()[ds(s * SEQ, SEQ), first * P:(first + count) * P]
            return bass.AP(tensor=v.tensor, offset=v.offset, ap=[[0, P]] + [list(d) for d in v.ap])

        def mod_tile(t, row, rows, b):
            at = (b * rows + row) * P
            return t[:, at:at + P]

        P1_LAG = 4

        def phase1(engine, step):
            for s in range(P1_LAG):
                step(s)
            with engine.Fori(P1_LAG, NG) as s:
                step(s, True)
            for s in range(NG, NG + P1_LAG):
                step(s)

        def has(s, g_lag, loop):
            return loop or 0 <= s - g_lag < NG

        def phase3(engine, step):
            step(0, True, False)
            with engine.Fori(1, NG) as s:
                step(s, True, True)
            step(NG, False, True)

        KS = UP + 2 * FFC
        UB = bank[4:8]

        def up_filled(s, k):
            return s * KS - UP + k + 1

        def up_emptied(s, k):
            return s * (KS // 2) - UP // 2 + k // 2 + 1

        @block.sync
        def _(sp):
            def row_copies(dst, first, count, partitions):
                src = bass.AP(tensor=rows.tensor, offset=first * P, ap=[[0, partitions], [1, count * P]])
                sp.dma_start(dst, src).then_inc(S["rows_in"], 16)

            sp.dma_start(cst[:, :], setup).then_inc(S["setup_in"], 16)
            sp.dma_start(wmod_sb, wmod).then_inc(S["wmod_in"], 16)
            row_copies(bias2, 0, 3, batch)
            row_copies(taps_row, 3, 3, P)
            sp.dma_start(win_sb[:, :], win).then_inc(S["win_in"], 16)
            sp.dma_start(res3[:, 0:P1_LAG * TILES, :], x_tok[:, 0:P1_LAG * TILES, :]).then_inc(S["x_in0"], 16)
            sp.dma_start(raw_sb, raw).then_inc(S["raw_in"], 16)
            sp.wait_ge(S["mod_ready"], 1)
            sp.dma_start(mod_dram.ap(), mod_sb).then_inc(S["mod_out"], 16)
            sp.wait_ge(S["mod_out"], 16)
            sp.dma_start(mod1[:, :], mod_rows(0, 2, 0)).then_inc(S["mod1_in"], 16)
            sp.dma_start(res3[:, P1_LAG * TILES:, :], x_tok[:, P1_LAG * TILES:, :]).then_inc(S["x_in1"], 16)
            sp.dma_start(w_sb[:, :], weights).then_inc(S["w_in"], 16)
            sp.dma_start(l3_sb[:, :], l3w).then_inc(S["w_in"], 16)
            sp.wait_ge(S["filt_ready"], 1)
            sp.dma_start(filt_dram.ap(), filt_p).then_inc(S["filt_out"], 16)
            sp.wait_ge(S["filt_out"], 16)

            def load_toeplitz(cg, slot):
                src = filt_dram.ap()[ds(cg * CG, CG), 0:1]
                rows = bass.AP(tensor=src.tensor, offset=src.offset, ap=[[1, P], [HW, CG * PARTS], [1, 2 * P]])
                dst = toep[:, slot * toep_w:(slot + 1) * toep_w].rearrange("p (r k) -> p r k", k=2 * P)
                sp.dma_start(dst, rows).then_inc(toep_in[slot], 16)

            for slot in range(SLOTS):
                load_toeplitz(slot, slot)

            def load_mod1(s):
                sp.wait_ge(S["h_s"], s)
                sp.dma_start(mod1[:, :], mod_rows(0, 2, s)).then_inc(S["mod1_in"], 16)

            with sp.Fori(1, NG) as s:
                load_mod1(s)

            with sp.Fori(1, NCG // SLOTS) as r:
                for slot in range(SLOTS):
                    sp.wait_ge(S["conv_mm"], (r - 1) * SLOTS + slot + 1)
                    load_toeplitz(r * SLOTS + slot, slot)

            sp.wait_ge(S["conv_mm"], NCG)
            sp.dma_start(xin3, x_tok[:, 0:TILES, :]).then_inc(S["xin_in"], 16)
            sp.dma_start(mod3[:, :], mod_rows(2, 4, 0)).then_inc(S["mod3_in"], 16)

            def step(s, mixer, ffn, last=False):
                if mixer and not last:
                    sp.wait_ge(S["xn_s"], s + 1)
                    sp.dma_start(xin3, x_tok[:, ds((s + 1) * TILES, TILES), :]).then_inc(S["xin_in"], 16)
                    sp.wait_ge(S["addb"], s + 1)
                    sp.dma_start(mod3[:, :], mod_rows(2, 4, s + 1)).then_inc(S["mod3_in"], 16)
                if ffn:
                    sp.wait_ge(S["fin"], s)
                    sp.dma_start(out_tok[:, ds((s - 1) * TILES, TILES), :], res3[:, ds((s - 1) * TILES, TILES), :]).then_inc(S["stored"], 16)
                if mixer:
                    if ffn:
                        sp.wait_ge(S["down_free"], s + 1)
                    sp.dma_start(modg[:, :], mod_rows(6, 1, s)).then_inc(S["modg_in"], 16)

            step(0, True, False)
            with sp.Fori(1, NG - 1) as s:
                step(s, True, True)
            step(NG - 1, True, True, last=True)
            step(NG, False, True)
            sp.wait_ge(S["stored"], 16 * NG)

        @block.scalar
        def _(act):
            act.wait_ge(S["setup_in"], 16)
            act.activation(silu_c[:, :], C("cT"), ACT.Silu).then_inc(S["silu"], 1)
            for n in range(poles):
                if n >= 4:
                    act.wait_ge(S["filt_acc"], n - 3)
                lp = C("log_poles")[:, n:n + 1]
                act.activation(decay[n % 4], C("time"), ACT.Exp, scale=lp).then_inc(S["decay_done"], 1)

            act.wait_ge(S["raw_in"], 16)
            l12, ups = slice(0, 2 * ff), slice(2 * ff, raw_w)
            act.activation(w_hi[:, l12], raw_sb[:, l12], ACT.Copy, scale=C("post_w"))
            act.activation(w_hi[:, ups], raw_sb[:, ups], ACT.Copy)
            act.wait_ge(S["gate_set"], 1)
            act.activation(w_hi[:, raw_w:], C("time")[:, 0:P], ACT.Identity, scale=0.0, bias=gate_diff[:, :]).then_inc(S["w_hi_s"], 1)

            def step(s, loop=False):
                if has(s, 3, loop):
                    for n, (k, dst) in enumerate(((1, acc1), (2, accv))):
                        hold(act, "z_s", (s - 3) * 2 + n + 1)
                        if has(s, 4, loop):
                            hold(act, "xvT_s", s - 3)
                        act.activation(dst[:, :], bank[1 + n][:, :], ACT.Identity, scale=C("short_w")[:, 3 * k + 2:3 * k + 3],
                                       bias=C("short_b")[:, k:k + 1]).then_inc(S["acc_s"], 1)
                    hold(act, "zx2_s", s - 2)
                    act.activation(x2T[:, ds((s - 3) * GT, GT)], bank[3][:, :], ACT.Identity,
                                   bias=C("short_b")[:, 0:1]).then_inc(S["x2_s"], 1)
                if has(s, 4, loop):
                    hold(act, "trx", s - 3)
                    act.activation(xv_part(0, s - 4), by_channel(bank[4][:, :]), ACT.Copy).then_inc(S["xv1_s"], 1)
                if has(s, 2, loop):
                    hold(act, "rms1_s", s - 1)
                    if has(s, 3, loop):
                        hold(act, "trh", s - 2)
                    for j in range(TILES):
                        i = act.activation(hnorm[:, j * P:(j + 1) * P], tok(s - 2, j), ACT.Copy, scale=rms[:, j:j + 1])
                    i.then_inc(S["hnorm_s"], 1)
                if has(s, 1, loop):
                    hold(act, "h_s", s)
                    for j in range(TILES):
                        i = act.activation(bank[7][:, j * P:(j + 1) * P], tok(s - 1, j), ACT.Square, accum_out=sumsq[:, j:j + 1])
                    i.then_inc(S["sumsq1_s"], 1)
                if has(s, 2, loop):
                    act.wait_ge(S["trh"], s - 1)
                    if has(s, 3, loop):
                        act.wait_ge(S["zx2_s"], s - 2)
                    act.activation(hT[:, :], bank[0][:, :], ACT.Copy).then_inc(S["hT_s"], 1)

            phase1(act, step)

            def put(cg, b):
                hold(act, "conv_mm", cg + 1)
                act.activation(y_all[:, ds(cg * (REG // 2), CG * NT)], bank[4 + b][:, :], ACT.Copy).then_inc(S["y_act"], 1)

            act.sem_inc(S["y_act"], 1)
            with act.Fori(0, NCG // SLOTS) as r:
                for b in range(0, SLOTS, 2):
                    put(r * SLOTS + b, b)

            def relu(s, k):
                act.wait_ge(S["up_mm"], up_filled(s, k))
                act.activation(hid[:, k * GT:(k + 1) * GT], UB[k % 4][:, :], ACT.Relu,
                               bias=W("up_b")[:, k:k + 1]).then_inc(S["up_act"], 1)

            def step3(s, mixer, ffn):
                if ffn:
                    relu(s, 0)
                    relu(s, 2)
                if mixer:
                    act.wait_ge(S["y2_s"], s + 1)
                    for j in range(TILES):
                        i = act.activation(junk2[:, j * P:(j + 1) * P], y2[:, j * P:(j + 1) * P], ACT.Square, accum_out=sumsq[:, j:j + 1])
                    i.then_inc(S["sumsq2"], 1)
                if ffn:
                    relu(s, 4)
                    relu(s, 6)
                if mixer:
                    act.wait_ge(S["rms2"], s + 1)
                    for j in range(TILES):
                        i = act.activation(znorm[:, j * P:(j + 1) * P], y2[:, j * P:(j + 1) * P], ACT.Copy, scale=rms[:, j:j + 1])
                    i.then_inc(S["znorm_s"], 1)
                if ffn:
                    relu(s, 8)
                if mixer:
                    act.wait_ge(S["trZ"], s + 1)
                    act.activation(zT[0][:, :], bank[1][:, :], ACT.Copy).then_inc(S["zT_hi"], 1)
                if ffn:
                    relu(s, 10)
                if mixer:
                    for n in range(FFC):
                        k = UP + 2 * n
                        act.wait_ge(S["up_mm"], up_filled(s, k))
                        act.activation(mlp[:, n * GT:(n + 1) * GT], UB[k % 4][0:FW, :], ACT.Gelu_apprx_tanh).then_inc(S["up_act"], 1)
                    act.wait_ge(S["trH"], s + 1)
                    act.activation(h2T[0][:, :], bank[1][:, :], ACT.Copy).then_inc(S["h2T_hi"], 1)

            phase3(act, step3)

        @block.vector
        def _(dve):
            dve.wait_ge(S["setup_in"], 16)
            dve.wait_ge(S["mod_mm"], 1)
            m = bank[5][0:batch, :]
            m2 = bank[6][0:batch, 0:2 * P]

            def row(n, count=1):
                return mod_sb[:, n * P:(n + count) * P]

            dve.wait_ge(S["rows_in"], 32)
            dve.tensor_scalar(row(0), m[:, P:2 * P], 1.0, None, ALU.add)
            dve.tensor_copy(row(1), m[:, 0:P])
            dve.tensor_scalar(row(3), m2[:, 0:P], 1.0, None, ALU.add)
            dve.tensor_copy(row(4), m[:, 3 * P:4 * P])
            dve.tensor_scalar(sign[:, 0:P], m[:, 2 * P:3 * P], 0.0, 2.0, ALU.is_ge, ALU.mult)
            dve.tensor_scalar(sign[:, P:2 * P], m2[:, P:2 * P], 0.0, 2.0, ALU.is_ge, ALU.mult)
            dve.tensor_copy(row(2), m[:, 2 * P:3 * P])
            dve.tensor_copy(row(6), m2[:, P:2 * P])
            dve.tensor_tensor(bias2[:, 0:P], bias2[:, 0:P], bias2[:, P:2 * P], ALU.add).then_inc(S["mod_a"], 1)
            dve.wait_ge(S["mod_a"], 1)
            dve.tensor_tensor(bias2[:, 0:P], bias2[:, 0:P], bias2[:, 2 * P:3 * P], ALU.add)
            dve.tensor_scalar(sign, sign, -1.0, None, ALU.add)
            for n in (2, 6):
                i = dve.scalar_tensor_tensor(row(n), row(n), -1.0, row(n), ALU.mult, ALU.max)
            i.then_inc(S["mod_b"], 1)
            dve.wait_ge(S["mod_b"], 1)
            for n, at_s in ((2, 0), (6, P)):
                i = dve.scalar_tensor_tensor(row(n), row(n), 0.25, sign[:, at_s:at_s + P], ALU.max, ALU.mult)
            i.then_inc(S["mod_c"], 1)
            dve.wait_ge(S["mod_c"], 1)
            dve.tensor_tensor(row(5), row(6), bias2[:, 0:P], ALU.mult).then_inc(S["mod_ready"], 1)

            for n in range(poles):
                dve.wait_ge(S["decay_done"], n + 1)
                r = C("residues")[:, n:n + 1]
                if n == 0:
                    dve.tensor_scalar(filt, decay[0], r, None, ALU.mult).then_inc(S["filt_acc"], 1)
                else:
                    dve.wait_ge(S["filt_acc"], n)
                    dve.scalar_tensor_tensor(filt, decay[n % 4], r, filt, ALU.mult, ALU.add).then_inc(S["filt_acc"], 1)
            dve.memset(filt_p, 0.0).then_inc(S["filt_d"], 1)
            dve.wait_ge(S["filt_acc"], poles)
            dve.tensor_tensor(filt[:, 0:1], filt[:, 0:1], C("d_skip"), ALU.add).then_inc(S["filt_d"], 1)
            dve.wait_ge(S["filt_d"], 2)
            taps = [filt_p[:, n * HW + P - 1:n * HW + P - 1 + length] for n in range(PARTS)]
            dve.tensor_copy(taps[0], filt).then_inc(S["filt_1"], 1)
            dve.wait_ge(S["filt_1"], 1)
            dve.tensor_tensor(filt_r, filt, taps[0], ALU.subtract).then_inc(S["filt_2"], 1)
            dve.wait_ge(S["filt_2"], 1)
            dve.tensor_copy(taps[1], filt_r).then_inc(S["filt_3"], 1)
            dve.wait_ge(S["filt_3"], 1)
            dve.tensor_tensor(taps[2], filt_r, taps[1], ALU.subtract).then_inc(S["filt_ready"], 1)
            dve.wait_ge(S["win_in"], 16)
            dve.tensor_scalar(win_sb[:, :], win_sb[:, :], C("pre_w"), None, ALU.mult).then_inc(S["win_scaled"], 1)
            dve.wait_ge(S["win_scaled"], 1)
            for k in range(3):
                i = dve.tensor_tensor(win_taps[:, k * P:(k + 1) * P], win_sb[:, 0:P], taps_row[:, k * P:(k + 1) * P], ALU.mult)
            i.then_inc(S["win_scaled"], 1)
            dve.tensor_tensor(gate_diff[:, :], C("gate")[:, 1:2], C("gate")[:, 0:1], ALU.subtract).then_inc(S["gate_set"], 1)
            dve.wait_ge(S["w_hi_s"], 1)
            high = w_hi[:, :].bitcast(F32)
            dve.scalar_tensor_tensor(w_lo[:, 0:2 * ff], raw_sb[:, 0:2 * ff], C("post_w"), high[:, 0:2 * ff], ALU.mult, ALU.subtract)
            dve.tensor_tensor(w_lo[:, 2 * ff:raw_w], raw_sb[:, 2 * ff:], high[:, 2 * ff:raw_w], ALU.subtract)
            dve.scalar_tensor_tensor(w_lo[:, raw_w:], high[:, raw_w:], -1.0, gate_diff[:, :].to_broadcast([P, P]),
                                     ALU.mult, ALU.add).then_inc(S["w_lo_s"], 1)
            dve.wait_ge(S["mod_out"], 16)
            dve.wait_ge(S["filt_out"], 16)

            def normalise(s, dst, cent, rows, scale_row, shift_row, tag):
                for j in range(TILES):
                    i = dve.scalar_tensor_tensor(cent[:, j * P:(j + 1) * P], tok(s, j), mv[:, 2 * j:2 * j + 1],
                                                 mod_tile(rows, scale_row[0], scale_row[1], j * P // length),
                                                 ALU.subtract, ALU.mult)
                i.then_inc(S[tag], 1)
                dve.wait_ge(S[tag], s + 1)
                for j in range(TILES):
                    i = dve.scalar_tensor_tensor(dst(j), cent[:, j * P:(j + 1) * P], rstd[:, j:j + 1],
                                                 mod_tile(rows, shift_row[0], shift_row[1], j * P // length),
                                                 ALU.mult, ALU.add)
                return i

            def statistics(s, bn, mvar):
                for j in range(TILES):
                    i = dve.bn_stats(stats[:, 6 * j:6 * j + 6], tok(s, j))
                i.then_inc(S[bn], 1)
                hold(dve, bn, s + 1)
                for j in range(TILES):
                    i = dve.bn_aggr(mv[:, 2 * j:2 * j + 2], stats[:, 6 * j:6 * j + 6])
                i.then_inc(S[mvar], 1)

            def step(s, loop=False):
                if has(s, 0, loop):
                    dve.wait_ge(S["x_in0"], 16)
                    if loop:
                        dve.wait_ge(S["x_in1"], 16)
                    statistics(s, "bn1", "mvar1")
                if has(s, 3, loop):
                    def tap(n, lag):
                        v = (acc1, accv)[n][:, :].rearrange("p (b t) -> p b t", t=length)[:, :, lag:length]
                        z = bank[1 + n][:, :].rearrange("p (b t) -> p b t", t=length)[:, :, 0:length - lag]
                        at = 3 * (n + 1) + 2 - lag
                        return dve.scalar_tensor_tensor(v, z, C("short_w")[:, at:at + 1], v, ALU.mult, ALU.add)
                    for n in range(2):
                        dve.wait_ge(S["acc_s"], (s - 3) * 2 + n + 1)
                        tap(n, 1).then_inc(S["tap1"], 1)
                    for n in range(2):
                        dve.wait_ge(S["tap1"], (s - 3) * 2 + n + 1)
                        tap(n, 2).then_inc(S["conv_s"], 1)
                if has(s, 4, loop):
                    dve.wait_ge(S["xv1_s"], s - 3)
                    dve.wait_ge(S["rest_free"], s - 3)
                    dve.tensor_tensor(packed(rest[:, :]), by_channel(bank[4][:, :]), xv_part(0, s - 4),
                                      ALU.subtract).then_inc(S["rest_s"], 1)
                if has(s, 0, loop):
                    dve.wait_ge(S["rstd1_s"], s + 1)
                    dve.wait_ge(S["mod1_in"], (s + 1) * 16)
                    normalise(s, lambda j: tok(s, j), cent1, mod1, (0, 2), (1, 2), "cent_s").then_inc(S["h_s"], 1)

            phase1(dve, step)

            def put(cg, b):
                dve.wait_ge(S["conv_mm"], cg + 1)
                dve.tensor_copy(y_all[:, ds(cg * (REG // 2), CG * NT)], bank[4 + b][:, :]).then_inc(S["y_dve"], 1)

            dve.sem_inc(S["y_dve"], 1)
            with dve.Fori(0, NCG // SLOTS) as r:
                for b in range(1, SLOTS, 2):
                    put(r * SLOTS + b, b)

            def relu(s, k):
                dve.wait_ge(S["up_mm"], up_filled(s, k))
                dve.tensor_scalar(hid[:, k * GT:(k + 1) * GT], UB[k % 4][:, :], W("up_b")[:, k:k + 1], 0.0,
                                  ALU.add, ALU.max).then_inc(S["up_dve"], 1)

            def per_sequence(t, row, rows):
                v = t[:, :].rearrange("p (b r c) -> p b r c", b=SEQ, r=rows)[:, :, row:row + 1, :]
                return v.to_broadcast([P, SEQ, TILES // SEQ, P])

            def tiles(ap):
                return ap.rearrange("p (b q c) -> p b q c", b=SEQ, c=P)

            def low_part(parts, src, done):
                dve.tensor_tensor(parts[1][:, :], src, parts[0][:, :].bitcast(F32), ALU.subtract).then_inc(S[done], 1)

            def step3(s, mixer, ffn):
                if mixer:
                    dve.wait_ge(S["trY"], s + 1)
                    dve.tensor_tensor(yx[:, :], bank[0][:, :], x2T[:, ds(s * GT, GT)], ALU.mult).then_inc(S["yx_s"], 1)
                if ffn:
                    dve.wait_ge(S["router"], s)
                    for h in range(2):
                        i = dve.scalar_tensor_tensor(h2T1[h][:, :], bank[2][:, :], 0.0, h2T[h][:, :].bitcast(F32), ALU.is_gt, ALU.mult)
                    i.then_inc(S["x1_s"], 1)
                    relu(s, 1)
                    relu(s, 3)
                if mixer:
                    dve.wait_ge(S["outp"], s + 1)
                    dve.tensor_tensor(y2[:, :], bank[2][:, :], group(s), ALU.add).then_inc(S["y2_s"], 1)
                if ffn:
                    for k in (5, 7, 9):
                        relu(s, k)
                if mixer:
                    dve.wait_ge(S["zT_hi"], s + 1)
                    low_part(zT, bank[1][:, :], "zT_lo")
                if ffn:
                    relu(s, 11)
                if mixer:
                    for n in range(FFC):
                        k = UP + 2 * n + 1
                        dve.wait_ge(S["up_mm"], up_filled(s, k))
                        dve.wait_ge(S["up_act"], up_emptied(s, k - 1))
                        m = mlp[:, n * GT:(n + 1) * GT]
                        dve.tensor_tensor(m, UB[k % 4][0:FW, :], m, ALU.mult).then_inc(S["up_dve"], 1)
                    dve.wait_ge(S["l3_mm"], s + 1)
                    dve.tensor_tensor(y2[:, :], bank[2][:, :], y2[:, :], ALU.add).then_inc(S["a_s"], 1)
                    dve.wait_ge(S["a_s"], s + 1)
                    dve.wait_ge(S["mod3_in"], (s + 1) * 16)
                    dve.tensor_tensor(tiles(y2[:, :]), tiles(y2[:, :]), per_sequence(mod3, 0, 4), ALU.mult).then_inc(S["ag_s"], 1)
                    dve.wait_ge(S["ag_s"], s + 1)
                    dve.wait_ge(S["xin_in"], (s + 1) * 16)
                    dve.tensor_tensor(group(s), y2[:, :], xin[:, :], ALU.add).then_inc(S["xn_s"], 1)
                    hold(dve, "xn_s", s + 1)
                    statistics(s, "bn2", "mvar2")
                    dve.wait_ge(S["rstd2_s"], s + 1)
                    normalise(s, lambda j: hn2[:, j * P:(j + 1) * P], cent2, mod3, (1, 4), (2, 4), "cent2_s").then_inc(S["h2_s"], 1)
                if ffn:
                    dve.wait_ge(S["down_mm"], s)
                    dve.wait_ge(S["modg_in"], s * 16)
                    dve.tensor_tensor(tiles(ffo[:, :]), tiles(bank[3][:, :]), per_sequence(modg, 0, 1), ALU.mult).then_inc(S["down_free"], 1)
                if mixer:
                    dve.wait_ge(S["h2T_hi"], s + 1)
                    low_part(h2T, bank[1][:, :], "h2T_lo")

            dve.sem_inc(S["down_free"], 1)
            phase3(dve, step3)

        @block.gpsimd
        def _(pool):
            pool.sem_inc(S["rest_free"], 1)
            pool.memset(half[:, :], -0.5).then_inc(S["half_set"], 1)
            pool.wait_ge(S["half_set"], 1)
            pool.wait_ge(S["mod_out"], 16)

            def inverse_root(dst, src, mul, eps, mid, done, n):
                pool.tensor_scalar(dst, src, mul, eps, ALU.mult, ALU.add).then_inc(S[mid], 1)
                pool.wait_ge(S[mid], n)
                pool.tensor_tensor(dst, dst, half[:, :], ALU.pow).then_inc(S[done], 1)

            var = mv[:, :].rearrange("p (j k) -> p j k", k=2)[:, :, 1]

            def step(s, loop=False):
                if has(s, 0, loop):
                    hold(pool, "mvar1", s + 1)
                    if has(s, 1, loop):
                        hold(pool, "h_s", s)
                    inverse_root(rstd[:, :], var, 1.0, LN_EPS, "veps1", "rstd1_s", s + 1)
                if has(s, 3, loop):
                    pool.wait_ge(S["conv_s"], (s - 2) * 2)
                    if has(s, 4, loop):
                        pool.wait_ge(S["trx"], s - 3)
                    a, v, dst = (t[:, :].rearrange("p (j t) -> p j t", t=P) for t in (acc1, accv, xvT))
                    pool.tensor_tensor(dst[:, :, ::-1], a, v, ALU.mult).then_inc(S["xvT_s"], 1)
                if has(s, 1, loop):
                    hold(pool, "sumsq1_s", s)
                    if has(s, 2, loop):
                        hold(pool, "hnorm_s", s - 1)
                    inverse_root(rms[:, :], sumsq[:, :], 1.0 / P, RMS_EPS, "meps1", "rms1_s", s)
                if has(s, 4, loop):
                    pool.wait_ge(S["rest_s"], s - 3)
                    pool.tensor_copy(xv_part(1, s - 4), packed(rest[:, :])).then_inc(S["xv2_s"], 1)
                    pool.wait_ge(S["xv2_s"], s - 3)
                    pool.tensor_tensor(xv_part(2, s - 4), packed(rest[:, :]), xv_part(1, s - 4), ALU.subtract).then_inc(S["rest_free"], 1)

            phase1(pool, step)

            def copy_y(s):
                pool.tensor_copy(by_channel(yc[:, :]), y_group(s)).then_inc(S["yc_s"], 1)

            pool.wait_ge(S["y_act"], NCG // 2 + 1)
            pool.wait_ge(S["y_dve"], NCG // 2 + 1)
            copy_y(0)

            def step3(s, mixer, ffn, last=False):
                if ffn:
                    pool.wait_ge(S["x1_s"], s)
                    for h in range(2):
                        i = pool.tensor_tensor(h2T0[h][:, :], h2T[h][:, :].bitcast(F32), h2T1[h][:, :].bitcast(F32), ALU.subtract)
                    i.then_inc(S["x0_s"], 1)
                if mixer:
                    hold(pool, "sumsq2", s + 1)
                    inverse_root(rms[:, :], sumsq[:, :], 1.0 / P, RMS_EPS, "meps2", "rms2", s + 1)
                    if not last:
                        pool.wait_ge(S["trY"], s + 1)
                        copy_y(s + 1)
                    hold(pool, "mvar2", s + 1)
                    inverse_root(rstd[:, :], var, 1.0, LN_EPS, "veps2", "rstd2_s", s + 1)
                    pool.wait_ge(S["h2_s"], s + 1)
                    for j in range(TILES):
                        i = pool.tensor_tensor(tok(s, j), tok(s, j), mod_tile(mod3, 3, 4, j * P // length), ALU.add)
                    i.then_inc(S["addb"], 1)
                if ffn:
                    pool.wait_ge(S["down_free"], s + 1)
                    pool.wait_ge(S["addb"], s)
                    pool.tensor_tensor(group(s - 1), group(s - 1), ffo[:, :], ALU.add).then_inc(S["fin"], 1)

            step3(0, True, False)
            with pool.Fori(1, NG - 1) as s:
                step3(s, True, True)
            step3(NG - 1, True, True, last=True)
            step3(NG, False, True)

        @block.tensor
        def _(pe):
            pe.wait_ge(S["silu"], 1)
            pe.wait_ge(S["wmod_in"], 16)
            pe.matmul(bank[5][0:batch, :], silu_c[:, :], wmod_sb[:, 0:512], start=True, stop=True)
            pe.matmul(bank[6][0:batch, 0:256], silu_c[:, :], wmod_sb[:, 512:768], start=True, stop=True).then_inc(S["mod_mm"], 1)
            pe.wait_ge(S["win_scaled"], 2)

            def transposes(dst, src):
                for j in range(TILES):
                    i = pe.transpose(dst[:, j * P:(j + 1) * P], src[:, j * P:(j + 1) * P], ident)
                return i

            def by_sequence(ap):
                return ap.rearrange("p (b t) -> p b t", t=length)

            def step(s, loop=False):
                if has(s, 2, loop):
                    pe.wait_ge(S["hnorm_s"], s - 1)
                    if has(s, 3, loop):
                        pe.wait_ge(S["hT_s"], s - 2)
                    transposes(bank[0], hnorm).then_inc(S["trh"], 1)
                    pe.wait_ge(S["hT_s"], s - 1)
                    for n, k in enumerate((1, 2)):
                        if has(s, 3, loop):
                            pe.wait_ge(S["conv_s"], (s - 3) * 2 + n + 1)
                        pe.matmul(bank[1 + n][:, :], win_sb[:, k * P:(k + 1) * P], hT[:, :], start=True, stop=True).then_inc(S["z_s"], 1)
                    if has(s, 3, loop):
                        pe.wait_ge(S["x2_s"], s - 2)
                    for lag in range(3):
                        i = pe.matmul(by_sequence(bank[3][:, :])[:, :, lag:], win_taps[:, (2 - lag) * P:(3 - lag) * P],
                                      by_sequence(hT[:, :])[:, :, 0:length - lag], start=lag == 0, stop=lag == 2,
                                      skip_group_check=True)
                    i.then_inc(S["zx2_s"], 1)
                if has(s, 3, loop):
                    pe.wait_ge(S["xvT_s"], s - 2)
                    if has(s, 4, loop):
                        pe.wait_ge(S["rest_s"], s - 3)
                    transposes(bank[4], xvT).then_inc(S["trx"], 1)

            phase1(pe, step)

            pe.wait_ge(S["rest_free"], NG + 1)
            with pe.Fori(0, NCG // SLOTS) as r:
                for slot in range(SLOTS):
                    pe.wait_ge(toep_in[slot], (r + 1) * 16)
                    if slot % 2 == 0:
                        pe.wait_ge(S["y_act"], r * 2 + slot // 2 + 1)
                    else:
                        pe.wait_ge(S["y_dve"], r * 2 + slot // 2 + 1)
                    dst = bank[4 + slot][:, :].rearrange("p (c b h) -> p c b h", c=CG, h=2)
                    for c in range(CG):
                        T = toep[:, slot * toep_w + c * PARTS * 2 * P:slot * toep_w + (c + 1) * PARTS * 2 * P]
                        first = True
                        for part_t in range(PARTS):
                            for part_x in range(PARTS - part_t):
                                at_x = (r * SLOTS + slot) * REG + part_x * CG * NT + c * NT
                                last = part_t == PARTS - 1
                                rows = xv[:, ds(at_x, NT)].rearrange("p (b h) -> p b h", h=2)
                                t0 = part_t * 2 * P
                                pe.matmul(dst[:, c, :, :], T[:, t0:t0 + P], rows, start=first, stop=False,
                                          skip_group_check=True)
                                i = pe.matmul(dst[:, c, :, 1], T[:, t0 + P:t0 + 2 * P], rows[:, :, 0], start=False,
                                              stop=last, skip_group_check=True)
                                first = False
                    i.then_inc(S["conv_mm"], 1)

            pe.wait_ge(S["w_lo_s"], 1)
            pe.wait_ge(S["w_in"], 32)

            def up_free(s, k):
                before = (s, k - 4) if k >= 4 else (s - 1, KS - 2 + k if k < 2 else KS - 6 + k)
                if isinstance(s, int) and s == 0 and k - 4 < UP:
                    return
                pe.wait_ge(S["up_act" if k % 2 == 0 else "up_dve"], up_emptied(*before))

            def split_matmul(dst, column, width, src):
                for w, x, first, last in ((w_hi, src[0], True, False), (w_hi, src[1], False, False), (w_lo, src[0], False, True)):
                    i = pe.matmul(dst, w[:, column:column + width], x[:, :], start=first, stop=last)
                return i

            def up(s, k, src):
                up_free(s, k)
                split_matmul(UB[k % 4][:, :], fc["up"][0] + k * P, P, src).then_inc(S["up_mm"], 1)

            def down(tile, done):
                for n in range(UP):
                    i = pe.matmul(bank[3][:, tile * P:(tile + 1) * P], hid[:, n * GT + tile * P:n * GT + (tile + 1) * P],
                                  W("down")[:, n * P:(n + 1) * P], start=n == 0, stop=n == UP - 1)
                if done:
                    i.then_inc(S["down_mm"], 1)

            def step3(s, mixer, ffn):
                if mixer:
                    pe.wait_ge(S["yc_s"], s + 1)
                    transposes(bank[0], yc).then_inc(S["trY"], 1)
                if ffn:
                    pe.wait_ge(S["h2T_hi"], s)
                    pe.wait_ge(S["h2T_lo"], s)
                    split_matmul(bank[2][:, :], fc["gate"][0], P, h2T).then_inc(S["router"], 1)
                    for k in range(0, 4):
                        up(s, k, h2T)
                    pe.wait_ge(S["x1_s"], s)
                if mixer:
                    pe.wait_ge(S["yx_s"], s + 1)
                    for j in range(TILES):
                        i = pe.matmul(bank[2][:, j * P:(j + 1) * P], yx[:, j * P:(j + 1) * P], W("out"), start=True, stop=True)
                    i.then_inc(S["outp"], 1)
                if ffn:
                    for k in range(4, 8):
                        up(s, k, h2T1)
                    pe.wait_ge(S["x0_s"], s)
                    for k in range(8, 10):
                        up(s, k, h2T0)
                if mixer:
                    pe.wait_ge(S["znorm_s"], s + 1)
                    transposes(bank[1], znorm).then_inc(S["trZ"], 1)
                if ffn:
                    for k in range(10, 12):
                        up(s, k, h2T0)
                if mixer:
                    pe.wait_ge(S["zT_hi"], s + 1)
                    pe.wait_ge(S["zT_lo"], s + 1)
                    for k in range(UP, KS):
                        n, name = (k - UP) // 2, ("l1", "l2")[(k - UP) % 2]
                        up_free(s, k)
                        split_matmul(UB[k % 4][0:FW, :], fc[name][0] + n * FW, FW, zT).then_inc(S["up_mm"], 1)
                if ffn:
                    pe.wait_ge(S["up_act"], up_emptied(s, UP - 2))
                    pe.wait_ge(S["up_dve"], up_emptied(s, UP - 1))
                    pe.wait_ge(S["down_free"], s)
                    down(0, False)
                if mixer:
                    pe.wait_ge(S["up_dve"], up_emptied(s, KS - 1))
                    for j in range(TILES):
                        for n in range(FFC):
                            i = pe.matmul(bank[2][:, j * P:(j + 1) * P], mlp[:, n * GT + j * P:n * GT + (j + 1) * P],
                                          l3_sb[:, n * P:(n + 1) * P], start=n == 0, stop=n == FFC - 1)
                    i.then_inc(S["l3_mm"], 1)
                if ffn:
                    down(1, False)
                    down(2, False)
                    down(3, True)
                if mixer:
                    pe.wait_ge(S["h2_s"], s + 1)
                    transposes(bank[1], hn2).then_inc(S["trH"], 1)

            phase3(pe, step3)


def kernel(**inputs):
    import numpy as np
    import concourse.bacc as bacc
    from concourse.bass_utils import run_bass_kernel_spmd

    a = {k.removeprefix("L0_"): np.asarray(v) for k, v in inputs.items()}
    u = a["attn_u"]
    batch, length, d = u.shape
    poles, ff, hidden = a["attn_residues"].shape[1], a["attn_l1_w"].shape[0], a["ffn_sw1"].shape[1]
    f = np.float32

    def chunks(w, rows):
        return w.reshape(-1, rows, w.shape[-1]).transpose(1, 0, 2).reshape(rows, -1)

    setup = np.concatenate([
        a["c"].T, a["attn_residues"], a["attn_log_poles"][:, :, 0], a["attn_D_skip"][:, None],
        chunks(a["attn_short_w"][:, 0, :], d), a["attn_short_b"].reshape(3, d).T, a["attn_pre_norm_w"][:, None],
        a["attn_post_norm_w"][:, None], a["ffn_gate_w"].T, np.eye(d, dtype=f),
        np.broadcast_to(np.arange(length, dtype=f), (d, length))], axis=1)
    downs = [a["ffn_sw2"], a["ffn_w2"][1], a["ffn_w2"][0]]
    up_b = [a["ffn_sb1"], a["ffn_b1"][1], a["ffn_b1"][0]]
    arrays = {
        "x": u.reshape(batch * length, d), "setup": setup, "wmod": a["wmod"], "win": a["attn_in_proj_w"].T,
        "weights": np.concatenate([a["attn_out_proj_w"].T] + [chunks(w, P) for w in downs]
                                  + [b.reshape(-1, P).T for b in up_b], axis=1),
        "raw": np.concatenate([a["attn_l1_w"].T, a["attn_l2_w"].T, a["ffn_sw1"], a["ffn_w1"][1], a["ffn_w1"][0]], axis=1),
        "l3w": chunks(a["attn_l3_w"].T, ff // 3),
        "rows": np.concatenate([a["ffn_b2"].reshape(-1), a["ffn_sb2"], a["attn_short_w"][:d, 0, :].T.reshape(-1)]),
    }
    arrays = {k: np.ascontiguousarray(v) for k, v in arrays.items()}
    nc = bacc.Bacc("TRN2", target_bir_lowering=False, num_devices=1)
    aps = {k: nc.dram_tensor(k, v.shape, mybir.dt.from_np(v.dtype), kind="ExternalInput").ap() for k, v in arrays.items()}
    out = nc.dram_tensor("out", (batch * length, d), F32, kind="ExternalOutput").ap()
    adaln_block(nc, *(aps[k] for k in ("x", "setup", "wmod", "win", "weights", "raw", "l3w", "rows")), out,
                batch, length, poles, ff, hidden)
    r = run_bass_kernel_spmd(nc, [arrays], core_ids=[0])
    return r.results[0]["out"].reshape(batch, length, d)
```

```python
from contextlib import ExitStack

import concourse.bass as bass
from concourse import mybir

F32 = mybir.dt.float32
F32R = mybir.dt.float32r
BF16 = mybir.dt.bfloat16
ALU = mybir.AluOpType
ACT = mybir.ActivationFunctionType
ds = bass.ds

P = 128
LN_EPS = 1e-5
RMS_EPS = 1e-6
TILES = 4
GT = TILES * P


def pack_columns(widths):
    at, out = 0, {}
    for name, w in widths:
        out[name] = (at, at + w)
        at += w
    return out, at


def setup_columns(batch, poles, length):
    return pack_columns([("cT", batch), ("residues", poles), ("log_poles", poles), ("d_skip", 1),
                         ("short_w", 9), ("short_b", 3), ("pre_w", 1), ("post_w", 1), ("gate", 2),
                         ("ident", P), ("time", length)])


def weight_columns(hidden):
    return pack_columns([("out", P), ("up_b", 3 * hidden // P)])


def split_columns(ff, hidden):
    return pack_columns([("l1", ff), ("l2", ff), ("up", 3 * hidden), ("gate", P)])


def adaln_block(nc, x, setup, wmod, win, weights, downs, raw, l3w, rows, out, batch, length, poles, ff, hidden):
    TOK = batch * length
    NG = TOK // GT
    NT = TOK // P
    SEQ = GT // length
    FFC = 3
    FW = ff // FFC
    HC = hidden // P
    UP = 3 * hidden // P
    CG = 8
    NCG = P // CG
    PARTS = 3
    REG = PARTS * CG * NT
    HW = 3 * P
    SLOTS = 5
    EARLY = SLOTS - 1
    HALF = CG // 2
    LAST = NCG - 1
    assert length == 2 * P and SEQ == 2 and ff % FFC == 0 and FW <= P and NCG % SLOTS == 1
    sc, setup_w = setup_columns(batch, poles, length)
    wc, weights_w = weight_columns(hidden)
    fc, split_w = split_columns(ff, hidden)
    raw_w = split_w - P
    MOD = 7
    RING = 4

    with ExitStack() as ctx:
        def sb(name, shape, dt=F32):
            return ctx.enter_context(nc.sbuf_tensor(name, shape, dt))

        def sem(name):
            return ctx.enter_context(nc.semaphore(name))

        bank = [ctx.enter_context(nc.psum_tensor(f"bank{i}", [P, 512], F32)) for i in range(8)]
        filt_dram = nc.dram_tensor("filter_parts", [P, PARTS * HW], BF16)
        mod_dram = nc.dram_tensor("modulation", [batch, 5 * P], F32)

        cst = sb("cst", [P, setup_w - length])
        w_sb = sb("w_sb", [P, weights_w])
        l3_sb = sb("l3_sb", [FW, FFC * P])
        w_hi = sb("w_hi", [P, split_w], F32R)
        w_lo = sb("w_lo", [P, split_w], F32R)
        res = sb("res", [P, TOK])
        x2T = sb("x2T", [P, TOK])
        xv = sb("xv", [P, NCG * REG], BF16)
        y_all = xv[:, :].bitcast(F32)
        half_w = HALF * PARTS * 2 * P
        stats = sb("stats", [P, TILES * 6])
        mv = sb("mv", [P, TILES * 2])
        rstd = sb("rstd", [P, TILES])
        sumsq = sb("sumsq", [P, TILES])
        rms = sb("rms", [P, TILES])
        half = sb("half", [P, TILES])
        gate_diff = sb("gate_diff", [P, 1])
        gelu_warm = sb("gelu_warm", [P, 1])
        gT = sb("gT", [P, 2 * batch])

        with ExitStack() as early:
            def sb1(name, width, dt=F32):
                return early.enter_context(nc.sbuf_tensor(name, [P, width], dt))

            toep_early = sb1("toep_early", EARLY * 2 * half_w, BF16)
            with ExitStack() as phase1_only:
                def sb0(name, width, dt=F32):
                    return phase1_only.enter_context(nc.sbuf_tensor(name, [P, width], dt))

                win_x1 = sb0("win_x1", P)
                win_taps = sb0("win_taps", 6 * P)
                silu_c = sb0("silu_c", batch)
                mod1 = sb0("mod1", SEQ * 2 * P)
                hT = [sb0(f"hT{i}", GT) for i in range(2)]
                hnorm, acc1, accv, xvT, rest = (sb0(n, GT) for n in ("hnorm", "acc1", "accv", "xvT", "rest"))
            toep_late = sb1("toep_late", 2 * half_w, BF16)
        hid_hi, hid_lo = (sb(f"hid_{h}", [P, RING * GT], F32R) for h in ("hi", "lo"))
        hid = sb("hid", [P, RING * GT])
        down_raw = hid[:, 0:UP * P]
        w_down = [sb(f"w_down_{h}", [P, UP * P], F32R) for h in ("hi", "lo")]
        mlp = sb("mlp", [FW, FFC * GT])
        yx, y2, yc, xin, ffoT, cent2 = (sb(n, [P, GT]) for n in ("yx", "y2", "yc", "xin", "ffoT", "cent2"))
        znorm = hn2 = yx
        zT, h2T, h2T1, h2T0 = ([sb(f"{n}_{h}", [P, GT], F32R) for h in ("hi", "lo")] for n in ("zT", "h2T", "h2T1", "h2T0"))
        mod3 = sb("mod3", [P, SEQ * 3 * P])
        g_now = sb("g_now", [P, 2 * SEQ])
        junk2 = sb("junk2", [P, GT], BF16)

        def C(name):
            return cst[:, sc[name][0]:sc[name][1]]

        def W(name):
            return w_sb[:, wc[name][0]:wc[name][1]]

        ident = C("ident")

        P1_LAG = 4

        wmod_at = TOK - raw_w - 6 * P
        filt_at = wmod_at - 3 * length - PARTS * HW // 2
        filt, filt_r, time = (x2T[:, filt_at + i * length:filt_at + (i + 1) * length] for i in range(3))
        filt_p = x2T[:, wmod_at - PARTS * HW // 2:wmod_at].bitcast(BF16)
        assert filt_at >= GT
        decay = [y_all[:, i * length:(i + 1) * length] for i in range(poles)]
        mod_at = poles * length
        mod_sb = y_all[0:batch, mod_at:mod_at + MOD * P]
        bias2 = y_all[0:batch, mod_at + MOD * P:mod_at + (MOD + 3) * P]
        sign = y_all[0:batch, mod_at + (MOD + 3) * P:mod_at + (MOD + 5) * P]
        taps_row = y_all[:, mod_at + (MOD + 5) * P:mod_at + (MOD + 11) * P]
        win_sb = y_all[:, mod_at + (MOD + 11) * P:mod_at + (MOD + 14) * P]
        raw_sb = x2T[:, TOK - raw_w:TOK]
        wmod_sb = x2T[:, TOK - raw_w - 6 * P:TOK - raw_w]

        names = """down_in setup_in time_in wmod_in win_in raw_in w_in x_in0 x_in1 x_in2 rows_in mod_out filt_out silu mod_mm mod01_ready mod01_out mod_a mod_b mod_c mod_ready
        half_set decay_done filt_acc filt_zero filt_sum filt_d filt_1 filt_2 filt_3 filt_ready win_scaled w_hi_s w_lo_s w_lo_pool gate_set
        mod1_in bn1 mvar1 veps1 rstd1_s cent_s h_s sumsq1_s meps1 rms1_s hnorm_s trh hT_s z_s zx2_s acc_s x2_s tap1 conv_s
        xvT_s trx xv1_s rest_s xv2_s rest_free
        conv_mm y_act y_dve
        yc_s trY yx_s up_mm up_act up_dve outp y2_s sumsq2 meps2 rms2 znorm_s trZ zT_hi zT_lo l3_mm xu_g xu_s ag_s xn_s
        gT_mm gT_s wd_hi wd_lo lo_dve lo_pool down_s ffoT_s trO g_now_s
        bn2 mvar2 veps2 rstd2_s cent2_s h2_s trH h2T_hi h2T_lo router x1_s x0_s fin
        xin_in mod3_in stored""".split()
        S = {n: sem(n) for n in names}
        toep_in = [sem(f"toep_in{i}") for i in range(2 * SLOTS)]

        passed = {str(e.engine): sem(f"passed{i}") for i, e in enumerate((nc.scalar, nc.vector, nc.gpsimd))}

        def toeplitz_half(i):
            t, at = (toep_early, i) if i < 2 * EARLY else (toep_late, i - 2 * EARLY)
            return t[:, at * half_w:(at + 1) * half_w]

        block = ctx.enter_context(nc.Block())
        x_tok = x.rearrange("(t p) c -> p t c", p=P)
        xin3 = xin[:, :].rearrange("p (t c) -> p t c", c=P)
        out_tok = out.rearrange("(t p) c -> p t c", p=P)
        res3 = res[:, :].rearrange("p (t c) -> p t c", c=P)

        def hold(engine, name, value):
            engine.wait_ge(S[name], value)
            engine.sem_inc(passed[str(engine.engine)], 1)

        def tok(s, j):
            return res[:, ds(s * GT + j * P, P)]

        def group(s):
            return res[:, ds(s * GT, GT)]

        def by_channel(ap):
            return ap.rearrange("p (j g c) -> p g c j", j=TILES, c=CG)

        def packed(ap):
            return ap.rearrange("p (g c j) -> p g c j", j=TILES, c=CG)

        def xv_part(n, s):
            v = xv[:, :].rearrange("p (g q) -> p g q", q=REG)[:, :, n * CG * NT:(n + 1) * CG * NT]
            return v.rearrange("p g (c t) -> p g c t", t=NT)[:, :, :, ds(s * TILES, TILES)]

        def y_group(s):
            v = y_all.rearrange("p (g q) -> p g q", q=REG // 2)[:, :, 0:CG * NT]
            return v.rearrange("p g (c t) -> p g c t", t=NT)[:, :, :, ds(s * TILES, TILES)]

        def mod_rows(first, count, s):
            v = mod_dram.ap()[ds(s * SEQ, SEQ), first * P:(first + count) * P]
            return bass.AP(tensor=v.tensor, offset=v.offset, ap=[[0, P]] + [list(d) for d in v.ap])

        def mod_tile(t, row, rows, b):
            at = (b * rows + row) * P
            return t[:, at:at + P]

        def per_sequence(t, row, rows):
            v = t[:, :].rearrange("p (b r c) -> p b r c", b=SEQ, r=rows)[:, :, row:row + 1, :]
            return v.to_broadcast([P, SEQ, TILES // SEQ, P])

        def tiles(ap):
            return ap.rearrange("p (b q c) -> p b q c", b=SEQ, c=P)

        def phase1(engine, step, setup_part=None):
            for s in range(P1_LAG):
                step(s, s % 2)
                if setup_part:
                    setup_part(s)
            with engine.Fori(P1_LAG // 2, NG // 2) as h:
                step(h * 2, 0, True)
                step(h * 2 + 1, 1, True)
            for s in range(NG, NG + P1_LAG):
                step(s, s % 2)

        def split_by_dve(g):
            return isinstance(g, int) and g >= NG - 2

        def split_rest(engine, g):
            engine.wait_ge(S["rest_s"], g + 2)
            engine.tensor_copy(xv_part(1, g), packed(rest[:, :])).then_inc(S["xv2_s"], 1)
            engine.wait_ge(S["xv2_s"], g + 1)
            engine.tensor_tensor(xv_part(2, g), packed(rest[:, :]), xv_part(1, g), ALU.subtract).then_inc(S["rest_free"], 1)

        def z_bank(n, odd_step, lag):
            return bank[(1, 5)[(odd_step + lag) % 2] + n]

        def has(s, g_lag, loop):
            return loop or 0 <= s - g_lag < NG

        def phase3(engine, step):
            step(0, True, False)
            step(1, True, True)
            with engine.Fori(2, NG) as s:
                step(s, True, True, done=True)
            step(NG, False, True, done=True)

        CB = bank[3:8]
        Y_ACT, Y_DVE = (SLOTS + 1) // 2, SLOTS // 2

        def all_y(engine):
            engine.wait_ge(S["y_act"], (NCG // SLOTS + 1) * Y_ACT + 1)
            engine.wait_ge(S["y_dve"], (NCG // SLOTS + 1) * Y_DVE)

        def copy_y(engine, s):
            engine.tensor_copy(by_channel(yc[:, :]), y_group(s)).then_inc(S["yc_s"], 1)

        BEFORE = 7
        MLP = 2 * FFC
        KS = UP + MLP
        UB = bank[4:8]
        L3B = (bank[0], bank[2])
        SQT = TILES // SEQ
        DVE_FULL = (1, 2, 3, 4, 5)
        LO_POOL = (9,)

        def ffn_place(k):
            return k if k < BEFORE else k + MLP

        FFN_PLACES = [ffn_place(k) for k in range(UP)]
        MLP_PLACES = [BEFORE + j for j in range(MLP)]
        ALL = sorted(FFN_PLACES + MLP_PLACES)
        BY_ACT = set(FFN_PLACES + MLP_PLACES[0::2])
        BY_DVE = set([ffn_place(k) for k in DVE_FULL] + MLP_PLACES[1::2])

        def places(s):
            if isinstance(s, int) and s == 0:
                return MLP_PLACES
            return FFN_PLACES if isinstance(s, int) and s == NG else ALL

        def count(kind, s, q):
            here = sum(1 for i in places(s) if i in kind and i <= q)
            if isinstance(s, int) and s == 0:
                return here
            return sum(1 for i in MLP_PLACES if i in kind) + (s - 1) * len(kind) + here

        def filled(s, q):
            return count(set(ALL), s, q)

        def same_bank_before(s, q):
            here = [i for i in places(s) if i < q and i % 4 == q % 4]
            if here:
                return s, here[-1]
            if isinstance(s, int) and s == 0:
                return None
            return s - 1, [i for i in places(s - 1) if i % 4 == q % 4][-1]

        def slot_used(s, k):
            return (s - 1) * UP + k - RING + 1

        LO_DVE = [k for k in range(UP) if k not in LO_POOL]

        def ring(t, k):
            return t[:, (k % RING) * GT:(k % RING + 1) * GT]

        def low_of_hidden(engine, s, k):
            engine.wait_ge(S["up_act"], count(BY_ACT, s, ffn_place(k)))
            engine.tensor_tensor(ring(hid_lo, k), ring(hid, k), ring(hid_hi, k).bitcast(F32),
                                 ALU.subtract).then_inc(S["lo_pool" if k in LO_POOL else "lo_dve"], 1)

        @block.sync
        def _(sp):
            def row_copies(dst, first, count, partitions):
                src = bass.AP(tensor=rows.tensor, offset=first * P, ap=[[0, partitions], [1, count * P]])
                sp.dma_start(dst, src).then_inc(S["rows_in"], 16)

            sp.dma_start(cst[:, :], setup[:, 0:setup_w - length]).then_inc(S["setup_in"], 16)
            sp.dma_start(wmod_sb, wmod).then_inc(S["wmod_in"], 16)
            sp.dma_start(time, setup[:, setup_w - length:]).then_inc(S["time_in"], 16)
            row_copies(bias2, 0, 3, batch)
            row_copies(taps_row, 3, 6, P)
            sp.dma_start(win_sb, win).then_inc(S["win_in"], 16)
            sp.dma_start(res3[:, 0:P1_LAG * TILES, :], x_tok[:, 0:P1_LAG * TILES, :]).then_inc(S["x_in0"], 16)
            sp.dma_start(raw_sb, raw).then_inc(S["raw_in"], 16)
            sp.wait_ge(S["mod01_ready"], 1)
            sp.dma_start(mod_dram.ap()[:, 0:2 * P], mod_sb[:, 0:2 * P]).then_inc(S["mod01_out"], 16)
            sp.wait_ge(S["mod01_out"], 16)
            sp.dma_start(mod1[:, :], mod_rows(0, 2, 0)).then_inc(S["mod1_in"], 16)
            sp.wait_ge(S["mod_ready"], 1)
            sp.dma_start(mod_dram.ap()[:, 2 * P:], mod_sb[:, 2 * P:5 * P]).then_inc(S["mod_out"], 16)

            def load_x(first, end, done):
                tiles_of = slice(first * TILES, end * TILES)
                sp.dma_start(res3[:, tiles_of, :], x_tok[:, tiles_of, :]).then_inc(S[done], 16)

            def load_mod1(s):
                sp.wait_ge(S["h_s"], s)
                sp.dma_start(mod1[:, :], mod_rows(0, 2, s)).then_inc(S["mod1_in"], 16)

            load_x(P1_LAG, 2 * P1_LAG, "x_in1")
            load_mod1(1)
            load_x(2 * P1_LAG, NG, "x_in2")
            load_mod1(2)
            sp.dma_start(w_sb[:, :], weights).then_inc(S["w_in"], 16)
            sp.dma_start(l3_sb[:, :], l3w).then_inc(S["w_in"], 16)
            load_mod1(3)
            sp.wait_ge(S["filt_ready"], 1)
            sp.dma_start(filt_dram.ap(), filt_p).then_inc(S["filt_out"], 16)
            sp.wait_ge(S["filt_out"], 16)

            def load_toeplitz(cg, slot, half):
                src = filt_dram.ap()[ds(cg * CG + half * HALF, HALF), 0:1]
                rows = bass.AP(tensor=src.tensor, offset=src.offset, ap=[[1, P], [HW, HALF * PARTS], [1, 2 * P]])
                dst = toeplitz_half(2 * slot + half).rearrange("p (r k) -> p r k", k=2 * P)
                sp.dma_start(dst, rows).then_inc(toep_in[2 * slot + half], 16)

            for slot in range(EARLY):
                load_mod1(P1_LAG + slot)
                for h in range(2):
                    load_toeplitz(slot, slot, h)
            with sp.Fori(P1_LAG + EARLY, NG) as s:
                load_mod1(s)
            sp.wait_ge(S["zx2_s"], NG)
            sp.wait_ge(S["xvT_s"], NG)
            for h in range(2):
                load_toeplitz(EARLY, EARLY, h)

            def refill(r, slot):
                for h in range(2):
                    sp.wait_ge(S["conv_mm"], ((r - 1) * SLOTS + slot) * 2 + h + 1)
                    load_toeplitz(r * SLOTS + slot, slot, h)

            with sp.Fori(1, NCG // SLOTS) as r:
                for slot in range(SLOTS):
                    refill(r, slot)
            refill(NCG // SLOTS, 0)

            sp.wait_ge(S["conv_mm"], 2 * LAST)
            sp.dma_start(down_raw, downs).then_inc(S["down_in"], 16)
            sp.dma_start(xin3, x_tok[:, 0:TILES, :]).then_inc(S["xin_in"], 16)
            sp.dma_start(mod3[:, :], mod_rows(2, 3, 0)).then_inc(S["mod3_in"], 16)

            def load(s):
                sp.wait_ge(S["xn_s"], SEQ * (s + 1))
                sp.dma_start(xin3, x_tok[:, ds((s + 1) * TILES, TILES), :]).then_inc(S["xin_in"], 16)
                sp.wait_ge(S["h2_s"], s + 1)
                sp.dma_start(mod3[:, :], mod_rows(2, 3, s + 1)).then_inc(S["mod3_in"], 16)

            def store(g):
                sp.wait_ge(S["fin"], g + 1)
                sp.dma_start(out_tok[:, ds(g * TILES, TILES), :], res3[:, ds(g * TILES, TILES), :]).then_inc(S["stored"], 16)

            load(0)
            load(1)
            with sp.Fori(2, NG - 1) as s:
                store(s - 2)
                load(s)
            for g in range(NG - 3, NG):
                store(g)
            sp.wait_ge(S["stored"], 16 * NG)

        @block.scalar
        def _(act):
            act.wait_ge(S["setup_in"], 16)
            act.activation(silu_c[:, :], C("cT"), ACT.Silu).then_inc(S["silu"], 1)
            act.wait_ge(S["time_in"], 16)
            for n in range(poles):
                lp = C("log_poles")[:, n:n + 1]
                act.activation(decay[n], time, ACT.Exp, scale=lp).then_inc(S["decay_done"], 1)

            act.wait_ge(S["raw_in"], 16)
            l12, ups = slice(0, 2 * ff), slice(2 * ff, raw_w)
            act.activation(w_hi[:, l12], raw_sb[:, l12], ACT.Copy, scale=C("post_w"))
            act.activation(w_hi[:, ups], raw_sb[:, ups], ACT.Copy)
            act.wait_ge(S["gate_set"], 1)
            act.activation(w_hi[:, raw_w:], ident, ACT.Identity, scale=0.0, bias=gate_diff[:, :]).then_inc(S["w_hi_s"], 1)

            def step(s, odd, loop=False):
                if has(s, 2, loop):
                    hold(act, "rms1_s", s - 1)
                    if has(s, 3, loop):
                        hold(act, "trh", s - 2)
                    for j in range(TILES):
                        i = act.activation(hnorm[:, j * P:(j + 1) * P], tok(s - 2, j), ACT.Copy, scale=rms[:, j:j + 1])
                    i.then_inc(S["hnorm_s"], 1)
                if has(s, 2, loop):
                    act.wait_ge(S["trh"], s - 1)
                    act.activation(hT[odd][:, :], bank[0][:, :], ACT.Copy).then_inc(S["hT_s"], 1)
                if has(s, 1, loop):
                    hold(act, "h_s", s)
                    for j in range(TILES):
                        i = act.activation(bank[7][:, j * P:(j + 1) * P], tok(s - 1, j), ACT.Square, accum_out=sumsq[:, j:j + 1])
                    i.then_inc(S["sumsq1_s"], 1)
                if has(s, 3, loop):
                    for n, (k, dst, scale) in enumerate(((1, acc1, C("short_w")[:, 5:6]), (2, accv, 1.0))):
                        hold(act, "z_s", (s - 3) * 2 + n + 1)
                        if has(s, 4, loop):
                            hold(act, "xvT_s", s - 3)
                        act.activation(dst[:, :], z_bank(n, odd, 3)[:, :], ACT.Identity, scale=scale,
                                       bias=C("short_b")[:, k:k + 1]).then_inc(S["acc_s"], 1)
                if has(s, 3, loop):
                    if loop:
                        act.wait_ge(S["filt_out"], 16)
                        act.wait_ge(S["w_lo_s"], 1)
                    hold(act, "zx2_s", s - 2)
                    act.activation(x2T[:, ds((s - 3) * GT, GT)], bank[3][:, :], ACT.Identity,
                                   bias=C("short_b")[:, 0:1]).then_inc(S["x2_s"], 1)
                if has(s, 4, loop):
                    hold(act, "trx", s - 3)
                    act.activation(xv_part(0, s - 4), by_channel(bank[4][:, :]), ACT.Copy).then_inc(S["xv1_s"], 1)

            def setup_part(s):
                if s == P1_LAG - 1:
                    act.wait_ge(S["mod01_out"], 16)
                    act.wait_ge(S["mod_out"], 16)
                    act.wait_ge(S["filt_d"], 1)
                    act.wait_ge(S["win_scaled"], 2)
                    act.wait_ge(S["w_lo_pool"], 1)

            phase1(act, step, setup_part)

            def put(cg, b):
                hold(act, "conv_mm", 2 * (cg + 1))
                act.activation(y_all[:, ds(cg * (REG // 2), CG * NT)], CB[b][:, :], ACT.Copy).then_inc(S["y_act"], 1)

            act.activation(gelu_warm[:, :], gate_diff[:, :], ACT.Gelu_apprx_tanh)
            act.sem_inc(S["y_act"], Y_ACT)
            with act.Fori(0, NCG // SLOTS) as r:
                for b in range(0, SLOTS, 2):
                    put(r * SLOTS + b, b)
            put(LAST, 0)

            act.wait_ge(S["w_in"], 32)
            act.wait_ge(S["down_in"], 16)
            act.activation(w_down[0][:, :], down_raw, ACT.Copy).then_inc(S["wd_hi"], 1)

            def relu(s, k):
                q = ffn_place(k)
                bias = W("up_b")[:, k:k + 1]
                if k in DVE_FULL:
                    act.wait_ge(S["up_dve"], count(BY_DVE, s, q))
                    act.activation(ring(hid_hi, k), ring(hid, k), ACT.Copy).then_inc(S["up_act"], 1)
                    return
                act.wait_ge(S["up_mm"], filled(s, q))
                if not (isinstance(s, int) and slot_used(s, k) <= 0):
                    act.wait_ge(S["down_s"], slot_used(s, k))
                act.activation(ring(hid, k), UB[q % 4][:, :], ACT.Relu, bias=bias)
                act.activation(ring(hid_hi, k), UB[q % 4][:, :], ACT.Relu, bias=bias).then_inc(S["up_act"], 1)

            def step3(s, mixer, ffn, done=False):
                if ffn:
                    relu(s, 0)
                if mixer:
                    act.wait_ge(S["y2_s"], s + 1)
                    for j in range(TILES):
                        i = act.activation(junk2[:, j * P:(j + 1) * P], y2[:, j * P:(j + 1) * P], ACT.Square, accum_out=sumsq[:, j:j + 1])
                    i.then_inc(S["sumsq2"], 1)
                if ffn:
                    relu(s, 1)
                    relu(s, 2)
                if mixer:
                    act.wait_ge(S["rms2"], s + 1)
                    for j in range(TILES):
                        i = act.activation(znorm[:, j * P:(j + 1) * P], y2[:, j * P:(j + 1) * P], ACT.Copy, scale=rms[:, j:j + 1])
                    i.then_inc(S["znorm_s"], 1)
                if ffn:
                    relu(s, 3)
                if mixer:
                    act.wait_ge(S["trZ"], s + 1)
                    act.activation(zT[0][:, :], bank[1][:, :], ACT.Copy).then_inc(S["zT_hi"], 1)
                if ffn:
                    for k in range(4, BEFORE):
                        relu(s, k)
                if mixer:
                    for n in range(FFC):
                        q = MLP_PLACES[2 * n]
                        act.wait_ge(S["up_mm"], filled(s, q))
                        act.activation(mlp[:, n * GT:(n + 1) * GT], UB[q % 4][0:FW, :], ACT.Gelu_apprx_tanh).then_inc(S["up_act"], 1)
                if ffn:
                    for k in range(BEFORE, UP):
                        relu(s, k)
                if mixer:
                    act.wait_ge(S["trH"], s + 1)
                    act.activation(h2T[0][:, :], bank[1][:, :], ACT.Copy).then_inc(S["h2T_hi"], 1)
                if ffn:
                    act.wait_ge(S["down_s"], s * UP)
                    act.wait_ge(S["g_now_s"], s)
                    for b in range(SEQ):
                        of_b = slice(b * length, (b + 1) * length)
                        i = act.activation(ffoT[:, of_b], bank[3][:, of_b], ACT.Identity, scale=g_now[:, 2 * b + 1:2 * b + 2],
                                           bias=g_now[:, 2 * b:2 * b + 1])
                    i.then_inc(S["ffoT_s"], 1)

            phase3(act, step3)

        @block.vector
        def _(dve):
            dve.wait_ge(S["setup_in"], 16)
            dve.tensor_tensor(gate_diff[:, :], C("gate")[:, 1:2], C("gate")[:, 0:1], ALU.subtract).then_inc(S["gate_set"], 1)
            dve.wait_ge(S["mod_mm"], 1)
            m = bank[5][0:batch, :]
            m2 = bank[6][0:batch, 0:2 * P]

            def row(n, count=1):
                return mod_sb[:, n * P:(n + count) * P]

            dve.tensor_scalar(row(0), m[:, P:2 * P], 1.0, None, ALU.add)
            dve.tensor_copy(row(1), m[:, 0:P]).then_inc(S["mod01_ready"], 1)
            dve.wait_ge(S["rows_in"], 32)
            dve.tensor_scalar(row(3), m2[:, 0:P], 1.0, None, ALU.add)
            dve.tensor_copy(row(4), m[:, 3 * P:4 * P])
            dve.tensor_scalar(sign[:, 0:P], m[:, 2 * P:3 * P], 0.0, 2.0, ALU.is_ge, ALU.mult)
            dve.tensor_scalar(sign[:, P:2 * P], m2[:, P:2 * P], 0.0, 2.0, ALU.is_ge, ALU.mult)
            dve.tensor_copy(row(2), m[:, 2 * P:3 * P])
            dve.tensor_copy(row(6), m2[:, P:2 * P])
            dve.tensor_tensor(bias2[:, 0:P], bias2[:, 0:P], bias2[:, P:2 * P], ALU.add).then_inc(S["mod_a"], 1)
            dve.wait_ge(S["mod_a"], 1)
            dve.tensor_tensor(bias2[:, 0:P], bias2[:, 0:P], bias2[:, 2 * P:3 * P], ALU.add)
            dve.tensor_scalar(sign, sign, -1.0, None, ALU.add)
            for n in (2, 6):
                i = dve.scalar_tensor_tensor(row(n), row(n), -1.0, row(n), ALU.mult, ALU.max)
            i.then_inc(S["mod_b"], 1)
            dve.wait_ge(S["mod_b"], 1)
            for n, at_s in ((2, 0), (6, P)):
                i = dve.scalar_tensor_tensor(row(n), row(n), 0.25, sign[:, at_s:at_s + P], ALU.max, ALU.mult)
            i.then_inc(S["mod_c"], 1)
            dve.wait_ge(S["mod_c"], 1)
            dve.tensor_tensor(row(5), row(6), bias2[:, 0:P], ALU.mult).then_inc(S["mod_ready"], 1)

            acc = (filt, filt_r)

            def sum_poles(first, end):
                for n in range(first, end):
                    dve.wait_ge(S["decay_done"], n + 1)
                    r = C("residues")[:, n:n + 1]
                    if n < 2:
                        dve.tensor_scalar(acc[n], decay[n], r, None, ALU.mult).then_inc(S["filt_acc"], 1)
                    else:
                        dve.wait_ge(S["filt_acc"], n - 1)
                        dve.scalar_tensor_tensor(acc[n % 2], decay[n], r, acc[n % 2], ALU.mult, ALU.add).then_inc(S["filt_acc"], 1)
                if end == poles:
                    dve.wait_ge(S["filt_acc"], poles)
                    dve.tensor_tensor(filt, filt, filt_r, ALU.add).then_inc(S["filt_sum"], 1)
                    dve.wait_ge(S["filt_sum"], 1)
                    dve.tensor_tensor(filt[:, 0:1], filt[:, 0:1], C("d_skip"), ALU.add).then_inc(S["filt_d"], 1)

            def scale_win():
                dve.wait_ge(S["win_in"], 16)
                dve.wait_ge(S["rows_in"], 32)
                dve.tensor_scalar(win_x1[:, :], win_sb[:, P:2 * P], C("pre_w"), None, ALU.mult).then_inc(S["win_scaled"], 1)
                for k in range(3):
                    for n, at_w in enumerate((0, 2 * P)):
                        at = (3 * n + k) * P
                        i = dve.scalar_tensor_tensor(win_taps[:, at:at + P], win_sb[:, at_w:at_w + P], C("pre_w"), taps_row[:, at:at + P],
                                                     ALU.mult, ALU.mult)
                i.then_inc(S["win_scaled"], 1)
                dve.wait_ge(S["gT_mm"], 1)
                for k in range(2):
                    i = dve.tensor_copy(gT[:, :].rearrange("p (b k) -> p k b", k=2)[:, k, :], bank[4][:, k * batch:(k + 1) * batch])
                i.then_inc(S["gT_s"], 1)

            def split_filter():
                taps = [filt_p[:, n * HW + P - 1:n * HW + P - 1 + length] for n in range(PARTS)]
                dve.wait_ge(S["filt_zero"], 1)
                dve.wait_ge(S["filt_d"], 1)
                dve.tensor_copy(taps[0], filt).then_inc(S["filt_1"], 1)
                dve.wait_ge(S["filt_1"], 1)
                dve.tensor_tensor(filt_r, filt, taps[0], ALU.subtract).then_inc(S["filt_2"], 1)
                dve.wait_ge(S["filt_2"], 1)
                dve.tensor_copy(taps[1], filt_r).then_inc(S["filt_3"], 1)
                dve.wait_ge(S["filt_3"], 1)
                dve.tensor_tensor(taps[2], filt_r, taps[1], ALU.subtract).then_inc(S["filt_ready"], 1)

            high = w_hi[:, :].bitcast(F32)

            def split_weights():
                dve.wait_ge(S["w_hi_s"], 1)
                dve.scalar_tensor_tensor(w_lo[:, 0:2 * ff], raw_sb[:, 0:2 * ff], C("post_w"), high[:, 0:2 * ff], ALU.mult, ALU.subtract)
                dve.scalar_tensor_tensor(w_lo[:, raw_w:], high[:, raw_w:], -1.0, gate_diff[:, :].to_broadcast([P, P]),
                                         ALU.mult, ALU.add).then_inc(S["w_lo_s"], 1)

            def normalise(s, dst, cent, rows, scale_row, shift_row, tag, rstd_tag, meanwhile=None):
                for j in range(TILES):
                    i = dve.scalar_tensor_tensor(cent(j), tok(s, j), mv[:, 2 * j:2 * j + 1],
                                                 mod_tile(rows, scale_row[0], scale_row[1], j * P // length),
                                                 ALU.subtract, ALU.mult)
                i.then_inc(S[tag], 1)
                if meanwhile:
                    meanwhile()
                dve.wait_ge(S[tag], s + 1)
                dve.wait_ge(S[rstd_tag], s + 1)
                for j in range(TILES):
                    i = dve.scalar_tensor_tensor(dst(j), cent(j), rstd[:, j:j + 1],
                                                 mod_tile(rows, shift_row[0], shift_row[1], j * P // length),
                                                 ALU.mult, ALU.add)
                return i

            def statistics(s, bn, mvar):
                for j in range(TILES):
                    i = dve.bn_stats(stats[:, 6 * j:6 * j + 6], tok(s, j))
                i.then_inc(S[bn], 1)
                aggregate(s, bn, mvar)

            def aggregate(s, bn, mvar):
                hold(dve, bn, s + 1)
                for j in range(TILES):
                    i = dve.bn_aggr(mv[:, 2 * j:2 * j + 2], stats[:, 6 * j:6 * j + 6])
                i.then_inc(S[mvar], 1)
                dve.wait_ge(S[mvar], s + 1)

            def step(s, odd, loop=False):
                if has(s, 0, loop) and not (isinstance(s, int) and s == 0):
                    dve.wait_ge(S["x_in0"], 16)
                    if loop:
                        dve.wait_ge(S["x_in1"], 16)
                        dve.wait_ge(S["x_in2"], 16)
                    statistics(s, "bn1", "mvar1")
                if has(s, 3, loop):
                    def tap(lag):
                        v = acc1[:, :].rearrange("p (b t) -> p b t", t=length)[:, :, lag:length]
                        z = z_bank(0, odd, 3)[:, :].rearrange("p (b t) -> p b t", t=length)[:, :, 0:length - lag]
                        return dve.scalar_tensor_tensor(v, z, C("short_w")[:, 5 - lag:6 - lag], v, ALU.mult, ALU.add)
                    dve.wait_ge(S["acc_s"], (s - 3) * 2 + 1)
                    tap(1).then_inc(S["tap1"], 1)
                    dve.wait_ge(S["tap1"], s - 2)
                    tap(2).then_inc(S["conv_s"], 1)
                if has(s, 4, loop):
                    dve.wait_ge(S["xv1_s"], s - 3)
                    dve.wait_ge(S["rest_free"], s - 3)
                    dve.tensor_tensor(packed(rest[:, :]), by_channel(bank[4][:, :]), xv_part(0, s - 4),
                                      ALU.subtract).then_inc(S["rest_s"], 1)
                    if split_by_dve(s - 4):
                        split_rest(dve, s - 4)
                if has(s, 0, loop):
                    dve.wait_ge(S["mod1_in"], (s + 1) * 16)
                    normalise(s, lambda j: tok(s, j), lambda j: tok(s, j), mod1, (0, 2), (1, 2), "cent_s", "rstd1_s").then_inc(S["h_s"], 1)

            EARLY_POLES = 6

            def setup_part(s):
                if s == 0:
                    sum_poles(0, EARLY_POLES)
                elif s == 1:
                    sum_poles(EARLY_POLES, poles)
                elif s == 2:
                    split_filter()
                else:
                    split_weights()

            dve.wait_ge(S["x_in0"], 16)
            statistics(0, "bn1", "mvar1")
            scale_win()
            dve.sem_inc(S["rest_s"], 1)
            phase1(dve, step, setup_part)

            def put(cg, b):
                dve.wait_ge(S["conv_mm"], 2 * (cg + 1))
                dve.tensor_copy(y_all[:, ds(cg * (REG // 2), CG * NT)], CB[b][:, :]).then_inc(S["y_dve"], 1)

            dve.sem_inc(S["y_dve"], Y_DVE)
            with dve.Fori(0, NCG // SLOTS) as r:
                for b in range(1, SLOTS, 2):
                    put(r * SLOTS + b, b)
            all_y(dve)
            copy_y(dve, 0)

            def relu(s, k):
                q = ffn_place(k)
                dve.wait_ge(S["up_mm"], filled(s, q))
                if not (isinstance(s, int) and slot_used(s, k) <= 0):
                    dve.wait_ge(S["down_s"], slot_used(s, k))
                dve.tensor_scalar(ring(hid, k), UB[q % 4][:, :], W("up_b")[:, k:k + 1], 0.0, ALU.add, ALU.max).then_inc(S["up_dve"], 1)

            def low_part(parts, src, done):
                dve.tensor_tensor(parts[1][:, :], src, parts[0][:, :].bitcast(F32), ALU.subtract).then_inc(S[done], 1)

            def finish(g):
                dve.wait_ge(S["trO"], g + 1)
                dve.tensor_tensor(group(g), group(g), bank[0][:, :], ALU.add).then_inc(S["fin"], 1)

            def step3(s, mixer, ffn, done=False):
                if mixer:
                    dve.wait_ge(S["trY"], s + 1)
                    dve.tensor_tensor(yx[:, :], bank[0][:, :], x2T[:, ds(s * GT, GT)], ALU.mult).then_inc(S["yx_s"], 1)
                if ffn:
                    dve.wait_ge(S["router"], s)
                    for h in range(2):
                        i = dve.scalar_tensor_tensor(h2T1[h][:, :], bank[1][:, :], 0.0, h2T[h][:, :].bitcast(F32), ALU.is_gt, ALU.mult)
                    i.then_inc(S["x1_s"], 1)
                if mixer:
                    dve.wait_ge(S["outp"], s + 1)
                    dve.tensor_tensor(y2[:, :], bank[2][:, :], group(s), ALU.add).then_inc(S["y2_s"], 1)
                if isinstance(s, int) and s == 0:
                    dve.wait_ge(S["wd_hi"], 1)
                    dve.tensor_tensor(w_down[1][:, :], down_raw, w_down[0][:, :].bitcast(F32), ALU.subtract).then_inc(S["wd_lo"], 1)
                if ffn:
                    low_of_hidden(dve, s, 0)
                    relu(s, 1)
                    for k in range(1, 4):
                        relu(s, k + 1)
                        low_of_hidden(dve, s, k)
                if mixer:
                    dve.wait_ge(S["zT_hi"], s + 1)
                    low_part(zT, bank[1][:, :], "zT_lo")
                if ffn:
                    relu(s, 5)
                    for k in range(4, BEFORE - 1):
                        low_of_hidden(dve, s, k)
                if done:
                    finish(s - 2)
                if mixer:
                    for n in range(FFC):
                        q = MLP_PLACES[2 * n + 1]
                        dve.wait_ge(S["up_mm"], filled(s, q))
                        dve.wait_ge(S["up_act"], count(BY_ACT, s, q))
                        m = mlp[:, n * GT:(n + 1) * GT]
                        dve.tensor_tensor(m, UB[q % 4][0:FW, :], m, ALU.mult).then_inc(S["up_dve"], 1)
                        if ffn and n == 0:
                            low_of_hidden(dve, s, BEFORE - 1)
                elif ffn:
                    low_of_hidden(dve, s, BEFORE - 1)
                if ffn:
                    low_of_hidden(dve, s, 7)
                if mixer:
                    dve.wait_ge(S["xu_s"], s + 1)

                    def add_mlp(b):
                        dve.wait_ge(S["ag_s"], SEQ * s + b + 1)
                        dve.tensor_tensor(res[:, ds(s * GT + b * length, length)], y2[:, b * length:(b + 1) * length],
                                          xin[:, b * length:(b + 1) * length], ALU.add).then_inc(S["xn_s"], 1)

                    for b in range(SEQ):
                        dve.wait_ge(S["l3_mm"], SEQ * s + b + 1)
                        dve.tensor_tensor(tiles(y2[:, :])[:, b], tiles(L3B[b][:, :])[:, b], per_sequence(mod3, 0, 3)[:, b],
                                          ALU.mult).then_inc(S["ag_s"], 1)
                        add_mlp(b)
                        hold(dve, "xn_s", SEQ * s + b + 1)
                        for j in range(b * SQT, (b + 1) * SQT):
                            i = dve.bn_stats(stats[:, 6 * j:6 * j + 6], tok(s, j))
                    i.then_inc(S["bn2"], 1)
                    aggregate(s, "bn2", "mvar2")
                    normalise(s, lambda j: hn2[:, j * P:(j + 1) * P], lambda j: cent2[:, j * P:(j + 1) * P], mod3, (1, 3), (2, 3),
                              "cent2_s", "rstd2_s", (lambda: low_of_hidden(dve, s, 8)) if ffn else None).then_inc(S["h2_s"], 1)
                elif ffn:
                    low_of_hidden(dve, s, 8)
                if ffn:
                    for k in (10, 11):
                        low_of_hidden(dve, s, k)
                if mixer:
                    dve.wait_ge(S["h2T_hi"], s + 1)
                    low_part(h2T, bank[1][:, :], "h2T_lo")

            phase3(dve, step3)
            finish(NG - 1)

        @block.gpsimd
        def _(pool):
            pool.sem_inc(S["rest_free"], 1)
            pool.memset(filt_p, 0.0).then_inc(S["filt_zero"], 1)
            pool.memset(half[:, :], -0.5).then_inc(S["half_set"], 1)
            pool.wait_ge(S["half_set"], 1)

            def inverse_root(dst, src, mul, eps, mid, done, n):
                pool.tensor_scalar(dst, src, mul, eps, ALU.mult, ALU.add).then_inc(S[mid], 1)
                pool.wait_ge(S[mid], n)
                pool.tensor_tensor(dst, dst, half[:, :], ALU.pow).then_inc(S[done], 1)

            var = mv[:, :].rearrange("p (j k) -> p j k", k=2)[:, :, 1]

            def rms_scale(s, loop):
                hold(pool, "sumsq1_s", s)
                if has(s, 2, loop):
                    hold(pool, "hnorm_s", s - 1)
                inverse_root(rms[:, :], sumsq[:, :], 1.0 / P, RMS_EPS, "meps1", "rms1_s", s)

            def step(s, odd, loop=False):
                if isinstance(s, int) and 0 < s < P1_LAG:
                    rms_scale(s, loop)
                if has(s, 0, loop):
                    hold(pool, "mvar1", s + 1)
                    if has(s, 1, loop):
                        hold(pool, "h_s", s)
                    inverse_root(rstd[:, :], var, 1.0, LN_EPS, "veps1", "rstd1_s", s + 1)
                if has(s, 1, loop) and not (isinstance(s, int) and s < P1_LAG):
                    rms_scale(s, loop)
                if has(s, 3, loop):
                    pool.wait_ge(S["conv_s"], s - 2)
                    pool.wait_ge(S["acc_s"], (s - 2) * 2)
                    if has(s, 4, loop):
                        pool.wait_ge(S["trx"], s - 3)
                    a, v, dst = (t[:, :].rearrange("p (j t) -> p j t", t=P) for t in (acc1, accv, xvT))
                    pool.tensor_tensor(dst[:, :, ::-1], a, v, ALU.mult).then_inc(S["xvT_s"], 1)
                if has(s, 4, loop) and not split_by_dve(s - 4):
                    split_rest(pool, s - 4)

            def setup_part(s):
                if s == 0:
                    pool.wait_ge(S["w_hi_s"], 1)
                    for at in range(2 * ff, raw_w, hidden):
                        i = pool.tensor_tensor(w_lo[:, at:at + hidden], raw_sb[:, at:at + hidden],
                                               w_hi[:, at:at + hidden].bitcast(F32), ALU.subtract)
                    i.then_inc(S["w_lo_pool"], 1)

            phase1(pool, step, setup_part)

            def step3(s, mixer, ffn, done=False, last=False):
                if mixer:
                    hold(pool, "sumsq2", s + 1)
                    inverse_root(rms[:, :], sumsq[:, :], 1.0 / P, RMS_EPS, "meps2", "rms2", s + 1)
                if ffn:
                    pool.wait_ge(S["x1_s"], s)
                    for h in range(2):
                        i = pool.tensor_tensor(h2T0[h][:, :], h2T[h][:, :].bitcast(F32), h2T1[h][:, :].bitcast(F32), ALU.subtract)
                    i.then_inc(S["x0_s"], 1)
                    if done:
                        pool.wait_ge(S["ffoT_s"], s - 1)
                    pool.tensor_copy(g_now[:, :], gT[:, ds((s - 1) * 2 * SEQ, 2 * SEQ)]).then_inc(S["g_now_s"], 1)
                if mixer:
                    pool.wait_ge(S["mod3_in"], (s + 1) * 16)
                    pool.wait_ge(S["xin_in"], (s + 1) * 16)
                    pool.tensor_tensor(tiles(cent2[:, :]), tiles(y2[:, :]), per_sequence(mod3, 0, 3), ALU.mult).then_inc(S["xu_g"], 1)
                    pool.wait_ge(S["xu_g"], s + 1)
                    pool.tensor_tensor(xin[:, :], xin[:, :], cent2[:, :], ALU.add).then_inc(S["xu_s"], 1)
                    if not last:
                        if isinstance(s, int) and s == 0:
                            all_y(pool)
                        pool.wait_ge(S["trY"], s + 1)
                        copy_y(pool, s + 1)
                    hold(pool, "mvar2", s + 1)
                    inverse_root(rstd[:, :], var, 1.0, LN_EPS, "veps2", "rstd2_s", s + 1)
                if ffn:
                    for k in LO_POOL:
                        low_of_hidden(pool, s, k)

            step3(0, True, False)
            step3(1, True, True)
            with pool.Fori(2, NG - 1) as s:
                step3(s, True, True, done=True)
            step3(NG - 1, True, True, done=True, last=True)
            step3(NG, False, True, done=True)

        @block.tensor
        def _(pe):
            pe.wait_ge(S["silu"], 1)
            pe.wait_ge(S["wmod_in"], 16)
            pe.matmul(bank[5][0:batch, :], silu_c[:, :], wmod_sb[:, 0:512], start=True, stop=True)
            pe.matmul(bank[6][0:batch, 0:256], silu_c[:, :], wmod_sb[:, 512:768], start=True, stop=True).then_inc(S["mod_mm"], 1)
            pe.wait_ge(S["mod_ready"], 1)
            for k, row in enumerate((5, 6)):
                i = pe.transpose(bank[4][:, k * batch:(k + 1) * batch], mod_sb[:, row * P:(row + 1) * P], ident[0:batch, 0:batch])
            i.then_inc(S["gT_mm"], 1)
            pe.wait_ge(S["win_scaled"], 2)
            pe.wait_ge(S["gT_s"], 1)

            def transposes(dst, src):
                for j in range(TILES):
                    i = pe.transpose(dst[:, j * P:(j + 1) * P], src[:, j * P:(j + 1) * P], ident)
                return i

            def by_sequence(ap):
                return ap.rearrange("p (b t) -> p b t", t=length)

            def with_taps(dst, h, first):
                for lag in range(3):
                    at = (first + 2 - lag) * P
                    i = pe.matmul(by_sequence(dst[:, :])[:, :, lag:], win_taps[:, at:at + P],
                                  by_sequence(h[:, :])[:, :, 0:length - lag], start=lag == 0, stop=lag == 2,
                                  skip_group_check=True)
                return i

            def step(s, odd, loop=False):
                if has(s, 2, loop):
                    pe.wait_ge(S["hnorm_s"], s - 1)
                    if has(s, 3, loop):
                        pe.wait_ge(S["hT_s"], s - 2)
                    transposes(bank[0], hnorm).then_inc(S["trh"], 1)
                if has(s, 4, loop):
                    pe.wait_ge(S["xvT_s"], s - 3)
                    pe.wait_ge(S["rest_s"], s - 3)
                    transposes(bank[4], xvT).then_inc(S["trx"], 1)
                if has(s, 3, loop):
                    if has(s, 4, loop):
                        pe.wait_ge(S["x2_s"], s - 3)
                    with_taps(bank[3], hT[1 - odd], 0).then_inc(S["zx2_s"], 1)
                if has(s, 2, loop):
                    pe.wait_ge(S["hT_s"], s - 1)
                    if has(s, 4, loop):
                        pe.wait_ge(S["conv_s"], s - 3)
                    pe.matmul(z_bank(0, odd, 2)[:, :], win_x1[:, :], hT[odd][:, :], start=True, stop=True).then_inc(S["z_s"], 1)
                    if has(s, 4, loop):
                        pe.wait_ge(S["acc_s"], (s - 3) * 2)
                    with_taps(z_bank(1, odd, 2), hT[odd], 3).then_inc(S["z_s"], 1)

            phase1(pe, step)

            pe.wait_ge(S["rest_free"], NG + 1)
            pe.wait_ge(S["x2_s"], NG)

            def bank_emptied(r, slot):
                if slot % 2 == 0:
                    pe.wait_ge(S["y_act"], r * Y_ACT + slot // 2 + 1)
                else:
                    pe.wait_ge(S["y_dve"], r * Y_DVE + slot // 2 + 1)

            def convolve(r, slot, last_one=False):
                dst = CB[slot][:, :].rearrange("p (c b h) -> p c b h", c=CG, h=2)
                for c in range(CG):
                    if c % HALF == 0:
                        pe.wait_ge(toep_in[2 * slot + c // HALF], (r + 1) * 16)
                    if c == HALF + 1 and not last_one:
                        bank_emptied(*((r, slot + 1) if slot + 1 < SLOTS else (r + 1, 0)))
                    T = toeplitz_half(2 * slot + c // HALF)
                    first = True
                    for part_t in range(PARTS):
                        for part_x in range(PARTS - part_t):
                            at_x = (r * SLOTS + slot) * REG + part_x * CG * NT + c * NT
                            last = part_t == PARTS - 1
                            rows = xv[:, ds(at_x, NT)].rearrange("p (b h) -> p b h", h=2)
                            t0 = ((c % HALF) * PARTS + part_t) * 2 * P
                            pe.matmul(dst[:, c, :, :], T[:, t0:t0 + P], rows, start=first, stop=False,
                                      skip_group_check=True)
                            i = pe.matmul(dst[:, c, :, 1], T[:, t0 + P:t0 + 2 * P], rows[:, :, 0], start=False,
                                          stop=last, skip_group_check=True)
                            first = False
                    if c % HALF == HALF - 1:
                        i.then_inc(S["conv_mm"], 1)

            bank_emptied(0, 0)
            with pe.Fori(0, NCG // SLOTS) as r:
                for slot in range(SLOTS):
                    convolve(r, slot)
            convolve(NCG // SLOTS, 0, last_one=True)

            pe.wait_ge(S["w_lo_s"], 1)
            pe.wait_ge(S["w_lo_pool"], 1)
            pe.wait_ge(S["w_in"], 32)

            def bank_free(s, q):
                before = same_bank_before(s, q)
                if before is None:
                    return
                if before[1] in BY_DVE:
                    pe.wait_ge(S["up_dve"], count(BY_DVE, *before))
                else:
                    pe.wait_ge(S["up_act"], count(BY_ACT, *before))

            def split_matmul(dst, column, width, src):
                for w, x, first, last in ((w_hi, src[0], True, False), (w_hi, src[1], False, False), (w_lo, src[0], False, True)):
                    i = pe.matmul(dst, w[:, column:column + width], x[:, :], start=first, stop=last)
                return i

            def up(s, first, end=None):
                for k in range(first, end or first + 1):
                    q = ffn_place(k)
                    bank_free(s, q)
                    split_matmul(UB[q % 4][:, :], fc["up"][0] + k * P, P, (h2T, h2T1, h2T0)[k // HC]).then_inc(S["up_mm"], 1)

            def down(s, k):
                if k in LO_POOL:
                    pe.wait_ge(S["lo_pool"], (s - 1) * len(LO_POOL) + LO_POOL.index(k) + 1)
                else:
                    pe.wait_ge(S["lo_dve"], (s - 1) * len(LO_DVE) + LO_DVE.index(k) + 1)
                hi, lo = (w[:, k * P:(k + 1) * P] for w in w_down)
                for w, x, n in ((hi, hid_hi, 0), (hi, hid_lo, 1), (lo, hid_hi, 2)):
                    i = pe.matmul(bank[3][:, :], w, ring(x, k), start=k == 0 and n == 0, stop=k == UP - 1 and n == 2)
                i.then_inc(S["down_s"], 1)

            def transpose_output(g):
                pe.wait_ge(S["ffoT_s"], g + 1)
                transposes(bank[0], ffoT).then_inc(S["trO"], 1)

            def step3(s, mixer, ffn, done=False):
                if mixer:
                    pe.wait_ge(S["yc_s"], s + 1)
                    transposes(bank[0], yc).then_inc(S["trY"], 1)
                if ffn:
                    pe.wait_ge(S["h2T_hi"], s)
                    pe.wait_ge(S["h2T_lo"], s)
                    split_matmul(bank[1][:, :], fc["gate"][0], P, h2T).then_inc(S["router"], 1)
                    up(s, 0)
                if mixer:
                    pe.wait_ge(S["yx_s"], s + 1)
                    for j in range(TILES):
                        i = pe.matmul(bank[2][:, j * P:(j + 1) * P], yx[:, j * P:(j + 1) * P], W("out"), start=True, stop=True)
                    i.then_inc(S["outp"], 1)
                if done:
                    transpose_output(s - 2)
                if ffn:
                    up(s, 1, 4)
                    if isinstance(s, int) and s == 1:
                        pe.wait_ge(S["wd_lo"], 1)
                    down(s, 0)
                    pe.wait_ge(S["x1_s"], s)
                    up(s, 4, 6)
                    down(s, 1)
                if mixer:
                    pe.wait_ge(S["znorm_s"], s + 1)
                    transposes(bank[1], znorm).then_inc(S["trZ"], 1)
                if ffn:
                    down(s, 2)
                    up(s, 6)
                    down(s, 3)
                if mixer:
                    pe.wait_ge(S["zT_hi"], s + 1)
                    pe.wait_ge(S["zT_lo"], s + 1)
                    for j, q in enumerate(MLP_PLACES):
                        n, name = j // 2, ("l1", "l2")[j % 2]
                        bank_free(s, q)
                        split_matmul(UB[q % 4][0:FW, :], fc[name][0] + n * FW, FW, zT).then_inc(S["up_mm"], 1)
                if ffn:
                    up(s, 7)
                    down(s, 4)
                if mixer:
                    pe.wait_ge(S["up_dve"], count(BY_DVE, s, MLP_PLACES[-1]))
                    if done:
                        pe.wait_ge(S["fin"], s - 1)
                    for j in range(TILES):
                        for n in range(FFC):
                            i = pe.matmul(L3B[j // SQT][:, j * P:(j + 1) * P], mlp[:, n * GT + j * P:n * GT + (j + 1) * P],
                                          l3_sb[:, n * P:(n + 1) * P], start=n == 0, stop=n == FFC - 1)
                        if j % SQT == SQT - 1:
                            i.then_inc(S["l3_mm"], 1)
                if ffn:
                    pe.wait_ge(S["x0_s"], s)
                    up(s, 8)
                    for k in (5, 6, 7):
                        down(s, k)
                        up(s, k + 4)
                    down(s, 8)
                    down(s, 9)
                if mixer:
                    pe.wait_ge(S["h2_s"], s + 1)
                    transposes(bank[1], hn2).then_inc(S["trH"], 1)
                if ffn:
                    down(s, 10)
                    down(s, 11)

            phase3(pe, step3)
            transpose_output(NG - 1)


def kernel(**inputs):
    import numpy as np
    import concourse.bacc as bacc
    from concourse.bass_utils import run_bass_kernel_spmd

    a = {k.removeprefix("L0_"): np.asarray(v) for k, v in inputs.items()}
    u = a["attn_u"]
    batch, length, d = u.shape
    poles, ff, hidden = a["attn_residues"].shape[1], a["attn_l1_w"].shape[0], a["ffn_sw1"].shape[1]
    f = np.float32

    def chunks(w, rows):
        return w.reshape(-1, rows, w.shape[-1]).transpose(1, 0, 2).reshape(rows, -1)

    setup = np.concatenate([
        a["c"].T, a["attn_residues"], a["attn_log_poles"][:, :, 0], a["attn_D_skip"][:, None],
        chunks(a["attn_short_w"][:, 0, :], d), a["attn_short_b"].reshape(3, d).T, a["attn_pre_norm_w"][:, None],
        a["attn_post_norm_w"][:, None], a["ffn_gate_w"].T, np.eye(d, dtype=f),
        np.broadcast_to(np.arange(length, dtype=f), (d, length))], axis=1)
    downs = [a["ffn_sw2"], a["ffn_w2"][1], a["ffn_w2"][0]]
    up_b = [a["ffn_sb1"], a["ffn_b1"][1], a["ffn_b1"][0]]
    arrays = {
        "x": u.reshape(batch * length, d), "setup": setup, "wmod": a["wmod"], "win": a["attn_in_proj_w"].T,
        "weights": np.concatenate([a["attn_out_proj_w"].T]
                                  + [b.reshape(-1, P).T for b in up_b], axis=1),
        "downs": np.concatenate([chunks(w, P) for w in downs], axis=1),
        "raw": np.concatenate([a["attn_l1_w"].T, a["attn_l2_w"].T, a["ffn_sw1"], a["ffn_w1"][1], a["ffn_w1"][0]], axis=1),
        "l3w": chunks(a["attn_l3_w"].T, ff // 3),
        "rows": np.concatenate([a["ffn_b2"].reshape(-1), a["ffn_sb2"], a["attn_short_w"][:d, 0, :].T.reshape(-1),
                                a["attn_short_w"][2 * d:, 0, :].T.reshape(-1)]),
    }
    arrays = {k: np.ascontiguousarray(v) for k, v in arrays.items()}
    nc = bacc.Bacc("TRN2", target_bir_lowering=False, num_devices=1)
    aps = {k: nc.dram_tensor(k, v.shape, mybir.dt.from_np(v.dtype), kind="ExternalInput").ap() for k, v in arrays.items()}
    out = nc.dram_tensor("out", (batch * length, d), F32, kind="ExternalOutput").ap()
    adaln_block(nc, *(aps[k] for k in ("x", "setup", "wmod", "win", "weights", "downs", "raw", "l3w", "rows")), out,
                batch, length, poles, ff, hidden)
    r = run_bass_kernel_spmd(nc, [arrays], core_ids=[0])
    return r.results[0]["out"].reshape(batch, length, d)
```
